# Optimizing a Trainium2 kernel written in Bass

```python
import numpy as np
import jax
import jax.numpy as jnp

def _softmax(x, axis=-1):
    return jax.nn.softmax(x, axis=axis)

def _gelu(x):
    return jax.nn.gelu(x, approximate=True)

def _silu(x):
    return jax.nn.silu(x)

def _sigmoid(x):
    return jax.nn.sigmoid(x)

def _layernorm(x, axis=-1, eps=1e-05):
    m = jnp.mean(x, axis=axis, keepdims=True)
    v = jnp.var(x, axis=axis, keepdims=True)
    return (x - m) / jnp.sqrt(v + eps)

def _scatter_add(tgt, idx, src, axis=0):
    return tgt.at[idx].add(src)

def _segment_sum(src, seg, n):
    return jax.ops.segment_sum(src, seg, n)
kernel_name = 'mk_macaron_d2_jaxref_r8_ade980'

def setup_inputs(seed: int=0):
    np.random.seed(seed)
    _w = jnp.asarray

    def _L0_attn_setup():
        import jax, jax.numpy as jnp
        import numpy as np
        D_MODEL = 256
        N_HEADS = 16
        HEAD_DIM = D_MODEL // N_HEADS
        B, T = (2, 256)
        key = jax.random.key(seed)
        ks = jax.random.split(key, 5)
        s = 0.02
        x = jax.random.normal(ks[0], (B, T, D_MODEL), dtype=jnp.float32)
        Wq = jax.random.normal(ks[1], (D_MODEL, D_MODEL), dtype=jnp.float32) * s
        Wk = jax.random.normal(ks[2], (D_MODEL, HEAD_DIM), dtype=jnp.float32) * s
        Wv = jax.random.normal(ks[3], (D_MODEL, HEAD_DIM), dtype=jnp.float32) * s
        Wo = jax.random.normal(ks[4], (D_MODEL, D_MODEL), dtype=jnp.float32) * s
        return {'x': x, 'Wq': Wq, 'Wk': Wk, 'Wv': Wv, 'Wo': Wo}
    _L0_attn_in = _L0_attn_setup()

    def _L0_ffn_setup():
        import jax, jax.numpy as jnp
        import numpy as np
        TOPK = 2
        N_EXPERTS = 8
        ROUTE_SCALE = 1.0
        key = jax.random.key(seed)
        ks = jax.random.split(key, 7)
        B, T, C = (4, 256, 256)
        H = 176
        HS = 352
        E = N_EXPERTS
        s = 0.02
        return {'x': jax.random.normal(ks[0], (B, T, C), jnp.float32), 'gate_w': jax.random.normal(ks[1], (E, C), jnp.float32) * s, 'gate_bias': jnp.zeros((E,), jnp.float32), 'shared_gw': jax.random.normal(ks[2], (2 * HS, C), jnp.float32) * s, 'shared_dw': jax.random.normal(ks[3], (C, HS), jnp.float32) * s, 'up_w': jax.random.normal(ks[4], (E, 2 * H, C), jnp.float32) * s, 'down_w': jax.random.normal(ks[5], (E, C, H), jnp.float32) * s}
    _L0_ffn_in = _L0_ffn_setup()

    def _L1_attn_setup():
        import jax, jax.numpy as jnp
        import numpy as np
        import math
        B_, L_, DM = (2, 256, 256)
        DI, DXB, N, DTR, K = (512, 128, 16, 128, 4)
        H = DI // N
        HXB = DXB // N
        REP = H // HXB
        key = jax.random.key(seed)
        ks = jax.random.split(key, 8)
        s = 0.02
        hidden_states = jax.random.normal(ks[0], (B_, L_, DM), jnp.float32)
        in_proj_w = jax.random.normal(ks[1], (2 * DXB + 2 * DI, DM), jnp.float32) * s
        dt_in_proj_w = jax.random.normal(ks[2], (DTR, DM), jnp.float32) * s
        dt_std = DTR ** (-0.5)
        dt_proj_w = jax.random.uniform(ks[3], (DI, DTR), jnp.float32, -dt_std, dt_std)
        dt = jnp.exp(jax.random.uniform(ks[4], (DI,), jnp.float32) * (math.log(0.1) - math.log(0.001)) + math.log(0.001))
        dt = jnp.clip(dt, 0.0001)
        dt_proj_b = dt + jnp.log(-jnp.expm1(-dt))
        conv_w = jax.random.normal(ks[5], (DI, K), jnp.float32) * s
        conv_b = jnp.zeros((DI,), jnp.float32)
        A_log = jnp.log(jnp.broadcast_to(jnp.arange(1, N + 1, dtype=jnp.float32), (DI, N)))
        D = jnp.ones((DI,), jnp.float32)
        out_proj_w = jax.random.normal(ks[6], (DM, DI), jnp.float32) * s
        return dict(hidden_states=hidden_states, in_proj_w=in_proj_w, dt_in_proj_w=dt_in_proj_w, dt_proj_w=dt_proj_w, dt_proj_b=dt_proj_b, conv_w=conv_w, conv_b=conv_b, A_log=A_log, D=D, out_proj_w=out_proj_w)
    _L1_attn_in = _L1_attn_setup()

    def _L1_ffn_setup():
        import jax, jax.numpy as jnp
        import numpy as np
        H = 256
        E = 64
        I = 64
        SI = 64
        TOP_K = 8
        B, T = (2, 64)
        key = jax.random.key(seed)
        ks = jax.random.split(key, 8)
        s = 0.02
        return {'h': jax.random.normal(ks[0], (B, T, H), jnp.float32), 'gate_w': jax.random.normal(ks[1], (E, H), jnp.float32) * s, 'gu_w': jax.random.normal(ks[2], (E, 2 * I, H), jnp.float32) * s, 'dp_w': jax.random.normal(ks[3], (E, H, I), jnp.float32) * s, 'sh_gate_w': jax.random.normal(ks[4], (SI, H), jnp.float32) * s, 'sh_up_w': jax.random.normal(ks[5], (SI, H), jnp.float32) * s, 'sh_down_w': jax.random.normal(ks[6], (H, SI), jnp.float32) * s, 'sh_gate1_w': jax.random.normal(ks[7], (1, H), jnp.float32) * s}
    _L1_ffn_in = _L1_ffn_setup()
    _d = {'L0_attn_x': _L0_attn_in['x'], 'L0_attn_Wq': _L0_attn_in['Wq'], 'L0_attn_Wk': _L0_attn_in['Wk'], 'L0_attn_Wv': _L0_attn_in['Wv'], 'L0_attn_Wo': _L0_attn_in['Wo'], 'L0_ffn_gate_w': _L0_ffn_in['gate_w'], 'L0_ffn_gate_bias': _L0_ffn_in['gate_bias'], 'L0_ffn_shared_gw': _L0_ffn_in['shared_gw'], 'L0_ffn_shared_dw': _L0_ffn_in['shared_dw'], 'L0_ffn_up_w': _L0_ffn_in['up_w'], 'L0_ffn_down_w': _L0_ffn_in['down_w'], 'L1_attn_in_proj_w': _L1_attn_in['in_proj_w'], 'L1_attn_dt_in_proj_w': _L1_attn_in['dt_in_proj_w'], 'L1_attn_dt_proj_w': _L1_attn_in['dt_proj_w'], 'L1_attn_dt_proj_b': _L1_attn_in['dt_proj_b'], 'L1_attn_conv_w': _L1_attn_in['conv_w'], 'L1_attn_conv_b': _L1_attn_in['conv_b'], 'L1_attn_A_log': _L1_attn_in['A_log'], 'L1_attn_D': _L1_attn_in['D'], 'L1_attn_out_proj_w': _L1_attn_in['out_proj_w'], 'L1_ffn_gate_w': _L1_ffn_in['gate_w'], 'L1_ffn_gu_w': _L1_ffn_in['gu_w'], 'L1_ffn_dp_w': _L1_ffn_in['dp_w'], 'L1_ffn_sh_gate_w': _L1_ffn_in['sh_gate_w'], 'L1_ffn_sh_up_w': _L1_ffn_in['sh_up_w'], 'L1_ffn_sh_down_w': _L1_ffn_in['sh_down_w'], 'L1_ffn_sh_gate1_w': _L1_ffn_in['sh_gate1_w']}
    _x0 = _d['L0_attn_x']
    _d['L0_attn_x'] = jax.random.normal(jax.random.fold_in(jax.random.key(seed), 1), (4, 512, 256), dtype=_x0.dtype)
    del _x0
    return _d

def reference(L0_attn_x, L0_attn_Wq, L0_attn_Wk, L0_attn_Wv, L0_attn_Wo, L0_ffn_gate_w, L0_ffn_gate_bias, L0_ffn_shared_gw, L0_ffn_shared_dw, L0_ffn_up_w, L0_ffn_down_w, L1_attn_in_proj_w, L1_attn_dt_in_proj_w, L1_attn_dt_proj_w, L1_attn_dt_proj_b, L1_attn_conv_w, L1_attn_conv_b, L1_attn_A_log, L1_attn_D, L1_attn_out_proj_w, L1_ffn_gate_w, L1_ffn_gu_w, L1_ffn_dp_w, L1_ffn_sh_gate_w, L1_ffn_sh_up_w, L1_ffn_sh_down_w, L1_ffn_sh_gate1_w):

    def _L0_attn_ref(x, Wq, Wk, Wv, Wo):
        import jax, jax.numpy as jnp
        import numpy as np
        D_MODEL = 256
        N_HEADS = 16
        HEAD_DIM = D_MODEL // N_HEADS
        B, T = (2, 256)
        Bx, Tx, Dx = x.shape
        scale = HEAD_DIM ** (-0.5)
        q = (x @ Wq).reshape(Bx, Tx, N_HEADS, HEAD_DIM).transpose(0, 2, 1, 3)
        k = x @ Wk
        v = x @ Wv
        attn = jnp.einsum('bhqd,bkd->bhqk', q, k) * scale
        causal = jnp.triu(jnp.ones((Tx, Tx), dtype=bool), k=1)
        attn = jnp.where(causal[None, None], -jnp.inf, attn)
        weights = jax.nn.softmax(attn, axis=-1)
        weights = jnp.nan_to_num(weights)
        out = jnp.einsum('bhqk,bkd->bhqd', weights, v)
        out = out.transpose(0, 2, 1, 3).reshape(Bx, Tx, Dx)
        return out @ Wo

    def _L0_ffn_ref(x, gate_w, gate_bias, shared_gw, shared_dw, up_w, down_w):
        import jax, jax.numpy as jnp
        import numpy as np
        TOPK = 2
        N_EXPERTS = 8
        ROUTE_SCALE = 1.0
        B, T, C = x.shape
        xf = x.reshape(-1, C)
        yg = xf @ shared_gw.T
        y, g = jnp.split(yg, 2, axis=-1)
        shared = jax.nn.silu(g) * y @ shared_dw.T
        scores = jax.nn.sigmoid(xf @ gate_w.T)
        _, topk_idx = jax.lax.top_k(scores + gate_bias, TOPK)
        w = jnp.take_along_axis(scores, topk_idx, axis=-1)
        w = w / jnp.sum(w, axis=-1, keepdims=True) * ROUTE_SCALE
        out = jnp.zeros_like(xf)
        for e in range(N_EXPERTS):
            we = jnp.sum(jnp.where(topk_idx == e, w, 0.0), axis=-1)
            gu = xf @ up_w[e].T
            g_e, u_e = jnp.split(gu, 2, axis=-1)
            h = jax.nn.silu(g_e) * u_e
            out = out + h @ down_w[e].T * we[:, None]
        return (shared + out).reshape(B, T, C)

    def _L1_attn_ref(hidden_states, in_proj_w, dt_in_proj_w, dt_proj_w, dt_proj_b, conv_w, conv_b, A_log, D, out_proj_w):
        import jax, jax.numpy as jnp
        import numpy as np
        import math
        B_, L_, DM = (2, 256, 256)
        DI, DXB, N, DTR, K = (512, 128, 16, 128, 4)
        H = DI // N
        HXB = DXB // N
        REP = H // HXB
        b, l, _ = hidden_states.shape
        zxbc = hidden_states @ in_proj_w.T
        z = zxbc[..., :DI]
        x = zxbc[..., DI:DI + DXB]
        Bmat = zxbc[..., DI + DXB:DI + 2 * DXB]
        C = zxbc[..., DI + 2 * DXB:]
        dt = hidden_states @ dt_in_proj_w.T @ dt_proj_w.T
        dt = jax.nn.softplus(dt + dt_proj_b)
        xh = jnp.repeat(x.reshape(b, l, HXB, N), REP, axis=2)
        xfull = xh.reshape(b, l, DI)
        xc = jnp.moveaxis(xfull, -1, 1)
        xp = jnp.pad(xc, ((0, 0), (0, 0), (K - 1, 0)))
        conv = sum((conv_w[None, :, k, None] * xp[:, :, k:k + l] for k in range(K)))
        xact = jax.nn.silu(conv + conv_b[None, :, None])
        xact = jnp.moveaxis(xact, 1, -1)
        Bh = jnp.repeat(Bmat.reshape(b, l, HXB, N), REP, axis=2)
        Ch = C.reshape(b, l, H, N)
        A = -jnp.exp(A_log).reshape(H, N, N)
        xh4 = xact.reshape(b, l, H, N)
        dth = dt.reshape(b, l, H, N)

        def step(h, inp):
            xt, dtt, Bt, Ct = inp
            dA = jnp.exp(dtt[..., None] * A)
            h = h * dA + (dtt * xt)[..., None] * Bt[:, :, None, :]
            yt = jnp.einsum('bhpn,bhn->bhp', h, Ct)
            return (h, yt)
        h0 = jnp.zeros((b, H, N, N), hidden_states.dtype)
        xs = (jnp.moveaxis(xh4, 1, 0), jnp.moveaxis(dth, 1, 0), jnp.moveaxis(Bh, 1, 0), jnp.moveaxis(Ch, 1, 0))
        _, ys = jax.lax.scan(step, h0, xs)
        y = jnp.moveaxis(ys, 0, 1).reshape(b, l, DI)
        y = (y + D * xact) * jax.nn.silu(z)
        return y @ out_proj_w.T

    def _L1_ffn_ref(h, gate_w, gu_w, dp_w, sh_gate_w, sh_up_w, sh_down_w, sh_gate1_w):
        import jax, jax.numpy as jnp
        import numpy as np
        H = 256
        E = 64
        I = 64
        SI = 64
        TOP_K = 8
        B, T = (2, 64)
        Bb, Tt, Hh = h.shape
        x = h.reshape(Bb * Tt, Hh)
        N = x.shape[0]
        logits = x @ gate_w.T
        topv, topi = jax.lax.top_k(logits, TOP_K)
        rw = jax.nn.softmax(topv.astype(jnp.float32), axis=-1).astype(x.dtype)
        W = jnp.zeros((N, E), x.dtype).at[jnp.arange(N)[:, None], topi].set(rw)
        gu = jnp.einsum('nh,eih->nei', x, gu_w)
        gate, up = (gu[..., :I], gu[..., I:])
        inter = jax.nn.silu(gate) * up
        inter_w = inter * W[:, :, None]
        out = jnp.einsum('nei,ehi->nh', inter_w, dp_w)
        sh_inter = jax.nn.silu(x @ sh_gate_w.T) * (x @ sh_up_w.T)
        sh_out = sh_inter @ sh_down_w.T
        sh_g = jax.nn.sigmoid(x @ sh_gate1_w.T)
        out = out + sh_g * sh_out
        return out.reshape(Bb, Tt, Hh)
    x = L0_attn_x
    x = x + 0.5 * _L0_ffn_ref(_layernorm(x, axis=-1), L0_ffn_gate_w, L0_ffn_gate_bias, L0_ffn_shared_gw, L0_ffn_shared_dw, L0_ffn_up_w, L0_ffn_down_w)
    x = x + _L0_attn_ref(_layernorm(x, axis=-1), L0_attn_Wq, L0_attn_Wk, L0_attn_Wv, L0_attn_Wo)
    x = x + 0.5 * _L0_ffn_ref(_layernorm(x, axis=-1), L0_ffn_gate_w, L0_ffn_gate_bias, L0_ffn_shared_gw, L0_ffn_shared_dw, L0_ffn_up_w, L0_ffn_down_w)
    x = x + 0.5 * _L1_ffn_ref(_layernorm(x, axis=-1), L1_ffn_gate_w, L1_ffn_gu_w, L1_ffn_dp_w, L1_ffn_sh_gate_w, L1_ffn_sh_up_w, L1_ffn_sh_down_w, L1_ffn_sh_gate1_w)
    x = x + _L1_attn_ref(_layernorm(x, axis=-1), L1_attn_in_proj_w, L1_attn_dt_in_proj_w, L1_attn_dt_proj_w, L1_attn_dt_proj_b, L1_attn_conv_w, L1_attn_conv_b, L1_attn_A_log, L1_attn_D, L1_attn_out_proj_w)
    x = x + 0.5 * _L1_ffn_ref(_layernorm(x, axis=-1), L1_ffn_gate_w, L1_ffn_gu_w, L1_ffn_dp_w, L1_ffn_sh_gate_w, L1_ffn_sh_up_w, L1_ffn_sh_down_w, L1_ffn_sh_gate1_w)
    return x

_drawn_inputs = setup_inputs


def setup_inputs(seed=0):
    import zlib

    import numpy as np

    out = dict(_drawn_inputs(seed))
    spreads = {'L0_ffn_gate_bias': (0.0, 0.8), 'L1_attn_conv_b': (0.0, 0.8), 'L1_attn_D': (1.0, 0.6)}
    factors = {'L0_attn_Wq': 8.0,
     'L0_attn_Wk': 8.0,
     'L0_attn_Wv': 4.704,
     'L0_attn_Wo': 4.681,
     'L0_ffn_gate_w': 8.0,
     'L0_ffn_shared_gw': 2.854,
     'L0_ffn_shared_dw': 2.86,
     'L0_ffn_up_w': 5.722,
     'L0_ffn_down_w': 5.73,
     'L1_attn_in_proj_w': 8.0,
     'L1_attn_dt_in_proj_w': 8.0,
     'L1_attn_dt_proj_w': 8.0,
     'L1_attn_dt_proj_b': 8.0,
     'L1_attn_conv_w': 8.0,
     'L1_attn_A_log': 8.0,
     'L1_attn_out_proj_w': 8.0,
     'L1_ffn_gate_w': 8.0,
     'L1_ffn_gu_w': 8.0,
     'L1_ffn_dp_w': 8.0,
     'L1_ffn_sh_gate_w': 8.0,
     'L1_ffn_sh_up_w': 8.0,
     'L1_ffn_sh_down_w': 8.0,
     'L1_ffn_sh_gate1_w': 8.0}
    for name, (base, spread) in spreads.items():
        noise = np.random.default_rng([zlib.crc32(name.encode()), seed]).standard_normal(out[name].shape)
        drawn = base * np.exp(spread * noise) if base else spread * noise
        out[name] = jnp.asarray(drawn.astype(out[name].dtype))
    for name, factor in factors.items():
        out[name] = (out[name] * factor).astype(out[name].dtype)
    return out
```

```python
from contextlib import ExitStack

import concourse.bass as bass
from concourse import mybir

P = 128
ALU = mybir.AluOpType
ACT = mybir.ActivationFunctionType
AX = mybir.AxisListType
F32 = mybir.dt.float32
F32R = mybir.dt.float32r
BF16 = mybir.dt.bfloat16
U32 = mybir.dt.uint32

NEG = -1.0e30
TAKEN = -3.0e38
RING = 2
WSLOTS = 4
DECAYS = 4


def split_rows(tile, rows, expert_rows, experts):
    lo, hi = tile * P, tile * P + P
    cut = next((e * expert_rows for e in range(1, experts + 1) if lo < e * expert_rows < hi), lo + 64)
    return [(0, cut - lo, min(lo // expert_rows, experts)), (cut - lo, P, min(cut // expert_rows, experts))]


def macaron_kernel(nc, a, out):
    NBATCH, SEQ, C = a["L0_attn_x"].shape
    KT = C // P
    NT = SEQ // P
    T = NBATCH * SEQ
    EPS = 1e-5
    HEADS = C // a["L0_attn_Wk"].shape[1]
    HD = a["L0_attn_Wk"].shape[1]
    SCALE = float(HD) ** -0.5
    HPT = P // HD
    E0, G0ROWS, _ = a["L0_ffn_up_w"].shape
    H0 = G0ROWS // 2
    HS = a["L0_ffn_shared_dw"].shape[1]
    TOP0 = 2
    ROWS0 = E0 * H0 + HS
    TILES0 = -(-ROWS0 // P)
    E1, G1ROWS, _ = a["L1_ffn_gu_w"].shape
    H1 = G1ROWS // 2
    PAIRS = E1 // 2
    TILES1 = PAIRS + 1
    R0, R1 = E0 + 1, E1 + 1
    DI, NST = a["L1_attn_A_log"].shape
    DXB = 128
    XH = DXB // NST
    REP = DI // DXB
    JT = DI // P
    OZ, OX, OB, OC = 0, DI, 2 * DI, 2 * DI + DXB
    WIN = OC + DI
    TAPS = a["L1_attn_conv_w"].shape[1]
    REC = 2 * KT * P + C
    assert (SEQ, C, KT, NT, HD, NST, JT, REP, H1, TOP0) == (512, 256, 2, 4, 16, 16, 4, 4, 64, 2)

    with ExitStack() as ctx:
        def sb(name, shape, dt=F32):
            return ctx.enter_context(nc.sbuf_tensor(name, shape, dt))

        def sem(name):
            return ctx.enter_context(nc.semaphore(name))

        wrec0 = nc.dram_tensor("wrec0", (TILES0, P, 2 * REC), F32, kind="Internal").ap()
        wrec1 = nc.dram_tensor("wrec1", (TILES1, P, 2 * REC), F32, kind="Internal").ap()
        route_t = nc.dram_tensor("route_t", (R1, T), F32, kind="Internal").ap()

        xT = sb("xT", [P, KT, NBATCH, SEQ])
        xn = sb("xn", [P, RING, KT, SEQ])
        sq = sb("sq", [P, RING, KT, SEQ])
        xnh = sb("xnh", [P, RING, KT, SEQ], F32R)
        xnl = sb("xnl", [P, RING, KT, SEQ], F32R)
        wslot = sb("wslot", [P, WSLOTS, 2, REC], F32R)
        iwh = sb("iwh", [P, RING, SEQ], F32R)
        iwl = sb("iwl", [P, RING, SEQ], F32R)
        bqh = sb("bqh", [2 * NST, JT, SEQ], F32R)
        bql = sb("bql", [2 * NST, JT, SEQ], F32R)
        sel_b = sb("sel_b", [2 * NST, NST, P], F32R)
        sel_c = sb("sel_c", [P, NST, P], F32R)
        w_in = sb("w_in", [P, KT, WIN])
        w_dtin = sb("w_dtin", [P, KT, P])
        w_dt = sb("w_dt", [P, DI])
        w_out = sb("w_out", [P, JT, C])
        wq = sb("wq", [P, KT, C])
        wk = sb("wk", [P, KT, HPT, HD])
        wv = sb("wv", [P, KT, HD])
        wo = sb("wo", [P, KT, C])
        gw0 = sb("gw0", [P, KT, E0])
        gw1 = sb("gw1", [P, KT, R1])
        ident = sb("ident", [P, P])
        ones = sb("ones", [P, P])
        identb = sb("identb", [P, P], BF16)
        maskb = sb("maskb", [P, P], BF16)
        zerob = sb("zerob", [P, SEQ], BF16)
        headmask = sb("headmask", [P, HPT])
        bias0 = sb("bias0", [P, E0])
        iota0 = sb("iota0", [P, E0])
        epsc = sb("epsc", [P, 1])
        conv_w = sb("conv_w", [P, JT, TAPS])
        conv_b = sb("conv_b", [P, JT])
        dt_b = sb("dt_b", [P, JT])
        d_skip = sb("d_skip", [P, JT])
        a_neg = sb("a_neg", [P, JT, NST])
        lg = sb("lg", [P, NT, R1])
        ex = sb("ex", [P, NT, R1])
        mk = sb("mk", [P, NT, R1])
        wr = sb("wr", [P, NT, R1])
        m8 = sb("m8", [P, NT, 8])
        ix = sb("ix", [P, NT, 8], U32)
        ixf = sb("ixf", [P, NT, TOP0])
        rsum = sb("rsum", [P, NT])
        mx = sb("mx", [P, RING, 2])
        nb = sb("nb", [P, RING, 2])
        psums = sb("psums", [P, NT, HEADS])
        pinv = sb("pinv", [P, NT, HEADS])
        vt = sb("vt", [P, NT, HD])
        tiny = sb("tiny", [P, 2])

        XPAD = SEQ + TAPS - 1
        ARENA = RING * XPAD + (NBATCH * KT + 6 * RING + DECAYS + 3) * SEQ
        arena = sb("arena", [P, ARENA])

        wts = [sq[:, c, 1, :] for c in range(RING)]

        def region(at, *dims):
            n = 1
            for d in dims:
                n *= d
            names = "abcd"[:len(dims)]
            v = arena[:, at:at + n]
            if len(dims) > 1:
                v = v.rearrange(f"p ({' '.join(names)}) -> p {' '.join(names)}",
                                **{k: d for k, d in zip(names[1:], dims[1:])})
            return v, at + n

        stage, o = region(0, WSLOTS, 3, C)
        st_in, o = region(o, 10, C)
        st_dtin, o = region(o, C)
        st_dt, o = region(o, JT, P)
        st_out, o = region(o, KT, DI)
        st_g0, o = region(o, C)
        st_g1, o = region(o, C)
        outbuf = region(0, 16, C)[0]
        xnat = xn[:, :, :, :].rearrange("p r k s -> p (r k s)")
        xnat2 = sq[:, :, :, :].rearrange("p r k s -> p (r k s)")
        qT, o = region(0, KT, SEQ)
        kpad, o = region(o, HPT, SEQ)
        prob, o = region(o, RING, SEQ)
        probT, o = region(o, RING, SEQ)
        osb, o = region(o, NT, C)
        oT, o = region(o, KT, SEQ)
        estage, o = region(o, WSLOTS, 3, C)
        assert o <= ARENA
        gact, o = region(0, RING, SEQ)
        prod, o = region(o, RING, SEQ)
        iw, o = region(o, RING, SEQ)
        wbc, o = region(o, RING, RING, SEQ)
        zg, o = region(0, RING, SEQ)
        xpad, o = region(o, RING, XPAD)
        xact, o = region(o, RING, SEQ)
        dt, o = region(o, RING, SEQ)
        sp_e, o = region(o, SEQ)
        sp_1, o = region(o, SEQ)
        sp_l, o = region(o, SEQ)
        da, o = region(o, DECAYS, SEQ)
        bx, o = region(o, RING, SEQ)
        hst, o = region(o, RING, SEQ)
        hc, o = region(o, RING, SEQ)
        xns, o = region(o, NBATCH, KT, SEQ)
        assert o == ARENA
        dtx = xpad[:, :, TAPS - 1:XPAD]
        bh_all = xnh[:, :, :, :].rearrange("p r k s -> p (r k) s")
        bl_all = xnl[:, :, :, :].rearrange("p r k s -> p (r k) s")
        dt_in = xn[:, :, :, :].rearrange("p r k s -> p (r k) s")

        ps = ctx.enter_context(nc.psum_tensor("ps", [P, 8, SEQ], F32))

        x_loaded = sem("x_loaded")
        w_loaded = sem("w_loaded")
        small_loaded = sem("small_loaded")
        consts = sem("consts")
        m_turned = sem("m_turned")
        small_ready = sem("small_ready")
        padded = sem("padded")
        attn_out = sem("attn_out")
        out_turned = sem("out_turned")
        m_kept = sem("m_kept")
        a_ready = sem("a_ready")
        stage_loaded = [sem(f"stage_loaded{i}") for i in range(WSLOTS)]
        rec_turned = sem("rec_turned")
        rec_hi = sem("rec_hi")
        rec_lo = sem("rec_lo")
        rec_stored = [sem(f"rec_stored{i}") for i in range(WSLOTS)]
        e_loaded = [sem(f"e_loaded{i}") for i in range(WSLOTS)]
        e_stored = [sem(f"e_stored{i}") for i in range(WSLOTS)]
        e_turned = sem("e_turned")
        e_hi = sem("e_hi")
        e_lo = sem("e_lo")
        mean_ready = sem("mean_ready")
        centred = sem("centred")
        squared = sem("squared")
        var_ready = sem("var_ready")
        log_done = sem("log_done")
        rstd_ready = sem("rstd_ready")
        xn_ready = sem("xn_ready")
        xn_hi = sem("xn_hi")
        xn_lo = sem("xn_lo")
        logits_ready = sem("logits_ready")
        route_dve = sem("route_dve")
        route_exp = sem("route_exp")
        route_ready = sem("route_ready")
        route_turned = sem("route_turned")
        route_kept = sem("route_kept")
        route_stored = sem("route_stored")
        wrec_in = [sem(f"wrec_in{i}") for i in range(WSLOTS)]
        wbc_in = [sem(f"wbc_in{i}") for i in range(RING)]
        gate_ready = sem("gate_ready")
        up_ready = sem("up_ready")
        silu_done = sem("silu_done")
        prod_done = sem("prod_done")
        weighted = sem("weighted")
        hid_hi = sem("hid_hi")
        hid_lo = sem("hid_lo")
        down_done = sem("down_done")
        ffn_out = sem("ffn_out")
        x_updated = sem("x_updated")
        qkv_ready = sem("qkv_ready")
        q_kept = sem("q_kept")
        k_kept = sem("k_kept")
        v_kept = sem("v_kept")
        score_ready = sem("score_ready")
        max_found = sem("max_found")
        negmax = sem("negmax")
        prob_ready = sem("prob_ready")
        prob_turned = sem("prob_turned")
        probT_kept = sem("probT_kept")
        pv_done = sem("pv_done")
        inv_ready = sem("inv_ready")
        o_normed = sem("o_normed")
        o_turned = sem("o_turned")
        o_kept = sem("o_kept")
        b_ready = sem("b_ready")
        b_hi = sem("b_hi")
        b_lo = sem("b_lo")
        dt_in_ready = sem("dt_in_ready")
        dt_in_kept = sem("dt_in_kept")
        bq_in = [sem(f"bq_in{j}") for j in range(JT)]
        proj_ready = sem("proj_ready")
        proj_taken = sem("proj_taken")
        conv_tap = sem("conv_tap")
        conv_done = sem("conv_done")
        conv_act = sem("conv_act")
        dt_abs = sem("dt_abs")
        dt_exp = sem("dt_exp")
        dt_one = sem("dt_one")
        dt_lost = sem("dt_lost")
        dt_log = sem("dt_log")
        dt_sum = sem("dt_sum")
        dt_done = sem("dt_done")
        dtx_done = sem("dtx_done")
        skip_set = sem("skip_set")
        c_lo = sem("c_lo")
        b_spread = sem("b_spread")
        c_spread = sem("c_spread")
        decay_ready = sem("decay_ready")
        bx_done = sem("bx_done")
        scanned = sem("scanned")
        hc_done = sem("hc_done")
        y_added = sem("y_added")
        y_gated = sem("y_gated")
        y_out = sem("y_out")
        stored = sem("stored")
        past_sp, past_pool, past_pe, past_dve = (sem(f"past_{e}") for e in ("sp", "pool", "pe", "dve"))
        act_own = sem("act_own")
        out_kept = sem("out_kept")

        block = ctx.enter_context(nc.Block())

        APP = NBATCH
        LN_RUNS = 6 * APP
        F0A, ATT, F0B, F1A, SSM, F1B = range(6)
        ROUTED = {F0A: 0, F0B: 1, F1A: 2, F1B: 3}
        TILES = {F0A: TILES0, F0B: TILES0, F1A: TILES1, F1B: TILES1}
        FFNS = [F0A, F0B, F1A, F1B]
        PAIRS_OF = NBATCH // 2
        NCONST = 25
        D0 = 18
        D1 = 15

        def tiles_before(layer, pr):
            return sum(PAIRS_OF * TILES[f] for f in FFNS if f < layer) + pr * TILES[layer]

        def slot_uses(layer, s):
            return len([t for t in range(TILES[layer]) if t % WSLOTS == s])

        def slot_count(layer, pr, s):
            return sum(PAIRS_OF * slot_uses(f, s) for f in FFNS if f < layer) + pr * slot_uses(layer, s)

        def ring_uses(layer, s):
            return len([t for t in range(TILES[layer]) if t % RING == s])

        def ring_count(layer, pr, s):
            return sum(PAIRS_OF * ring_uses(f, s) for f in FFNS if f < layer) + pr * ring_uses(layer, s)

        def dve_route_before(layer, chunk):
            n = 0
            for f in FFNS:
                if f < layer:
                    n = n + NBATCH * (D0 if f in (F0A, F0B) else D1)
            return n + chunk * (D0 if layer in (F0A, F0B) else D1)

        def ROUTED_EXP(layer, chunk):
            return ROUTED[layer] * NBATCH + chunk

        def x_before(layer):
            return KT * NBATCH * (layer + (JT - 1 if layer > SSM else 0))

        JOBS = 4
        STEPS = JT * NST
        NPREP = TILES0 + 1
        EPB = PAIRS // NBATCH

        def weight_pieces(g):
            if g == TILES0:
                return [(0, H1, a["L1_ffn_sh_gate_w"], a["L1_ffn_sh_up_w"], a["L1_ffn_sh_down_w"])]
            found, r, end = [], g * P, min(g * P + P, ROWS0)
            up, down = a["L0_ffn_up_w"], a["L0_ffn_down_w"]
            shared, sdown = a["L0_ffn_shared_gw"], a["L0_ffn_shared_dw"]
            while r < end:
                e = min(r // H0, E0)
                i = r - e * H0
                m = min((H0 if e < E0 else HS) - i, end - r)
                if e < E0:
                    w = up[e, i:i + m, :], up[e, H0 + i:H0 + i + m, :], down[e, :, i:i + m]
                else:
                    w = shared[HS + i:HS + i + m, :], shared[i:i + m, :], sdown[:, i:i + m]
                found.append((r - g * P, r - g * P + m, *w))
                r += m
            return found

        def padding(g):
            return {TILES0 - 1: ROWS0 - P * (TILES0 - 1), NPREP - 1: H1}.get(g, P)

        def stage_count(g):
            return 48 * sum(len(weight_pieces(x)) for x in range(g % WSLOTS, g + 1, WSLOTS))


        @block.sync
        def _(sp):
            xr = a["L0_attn_x"].rearrange("b (t p) c -> p (b t) c", p=P)
            sp.dma_start(xnat[:, :].rearrange("p (t c) -> p t c", c=C), xr[:, 0:8, :]).then_inc(x_loaded, 16)
            sp.dma_start(xnat2[:, :].rearrange("p (t c) -> p t c", c=C), xr[:, 8:16, :]).then_inc(x_loaded, 16)
            sp.dma_start(st_in, a["L1_attn_in_proj_w"].rearrange("(r p) c -> p r c", p=P)).then_inc(w_loaded, 16)
            sp.dma_start(st_dtin, a["L1_attn_dt_in_proj_w"]).then_inc(w_loaded, 16)
            sp.dma_start(st_dt, a["L1_attn_dt_proj_w"].rearrange("(j p) c -> p j c", p=P)).then_inc(w_loaded, 16)
            sp.dma_start(st_out, a["L1_attn_out_proj_w"].rearrange("(k p) c -> p k c", p=P)).then_inc(w_loaded, 16)
            sp.dma_start(st_g0[0:E0, :], a["L0_ffn_gate_w"]).then_inc(w_loaded, 16)
            sp.dma_start(st_g1[0:E1, :], a["L1_ffn_gate_w"]).then_inc(w_loaded, 16)
            sp.dma_start(st_g1[E1:R1, :], a["L1_ffn_sh_gate1_w"]).then_inc(w_loaded, 16)

            def store_record(g):
                sp.wait_ge(rec_lo, g + 1 + RING)
                dst = wrec0[g] if g < TILES0 else wrec1[PAIRS]
                sp.dma_start(dst, wslot[:, g % WSLOTS, :, :].rearrange("p h w -> p (h w)").bitcast(F32)
                             ).then_inc(rec_stored[g % WSLOTS], 16)

            for g in range(NPREP):
                s = g % WSLOTS
                if g >= WSLOTS:
                    sp.wait_ge(rec_turned, g - WSLOTS + 1)
                for first, end, gate, up, down in weight_pieces(g):
                    dst = stage[:, s, 2, :].rearrange("p (k r) -> p k r", k=KT)[:, :, first:end]
                    sp.dma_start(stage[first:end, s, 0, :], gate).then_inc(stage_loaded[s], 16)
                    sp.dma_start(stage[first:end, s, 1, :], up).then_inc(stage_loaded[s], 16)
                    sp.dma_start(dst, down.rearrange("(k p) r -> p k r", p=P)).then_inc(stage_loaded[s], 16)
                if g >= WSLOTS:
                    store_record(g - WSLOTS)
            for g in range(NPREP - WSLOTS, NPREP):
                store_record(g)
            for s in range(WSLOTS):
                sp.wait_ge(rec_stored[s], 16 * len(range(s, NPREP, WSLOTS)))
            sp.sem_inc(route_stored, 16)
            for s in range(WSLOTS):
                sp.sem_inc(e_stored[s], 16)

            def route_out(layer, c, chunk, routed):
                sp.wait_ge(route_kept, routed + 1)
                sp.sem_inc(past_sp, 1)
                rows = R0 if layer in (F0A, F0B) else R1
                sp.dma_start(route_t.rearrange("r (b s) -> r b s", s=SEQ)[0:rows, chunk, :],
                             wts[c][0:rows, :]).then_inc(route_stored, 16)
                sp.wait_ge(route_stored, 16 * routed + 32)
                sp.sem_inc(past_sp, 1)

            def load_tile(layer, pr, t, s, r, g, pieces, first):
                src = wrec0 if layer in (F0A, F0B) else wrec1
                if first is None or first >= WSLOTS:
                    sp.wait_ge(down_done, 2 * (g - WSLOTS + 1) + RING)
                    sp.sem_inc(past_sp, 1)
                sp.dma_start(wslot[:, s, :, :].rearrange("p h w -> p (h w)").bitcast(F32), src[bass.ds(t, 1), :, :].rearrange("t p w -> (t p) w")).then_inc(wrec_in[s], 16)
                if first is None or first >= RING:
                    sp.wait_ge(weighted, 2 * (g - RING + 1) + RING)
                    sp.sem_inc(past_sp, 1)
                for lo, hi, row in pieces:
                    src = route_t.rearrange("r (q s) -> r q s", s=SEQ)[bass.ds(row, 1), bass.ds(2 * pr, 2), :]
                    sp.dma_start(wbc[lo:hi, r, :, :], src.broadcast_to([hi - lo, 2, SEQ])).then_inc(wbc_in[r], 16)

            def ffn(layer):
                with sp.Fori(0, PAIRS_OF) as pr:
                    base = tiles_before(layer, pr)
                    for c in range(2):
                        route_out(layer, c, 2 * pr + c, ROUTED[layer] * NBATCH + 2 * pr + c)
                    sp.wait_ge(down_done, 2 * base + RING)
                    sp.sem_inc(past_sp, 1)
                    if layer in (F0A, F0B):
                        for t in range(TILES0):
                            load_tile(layer, pr, t, t % WSLOTS, t % RING, base + t, split_rows(t, ROWS0, H0, E0), t)
                    else:
                        with sp.Fori(0, PAIRS // WSLOTS) as i:
                            for u in range(WSLOTS):
                                t = WSLOTS * i + u
                                load_tile(layer, pr, t, u, u % RING, base + t, [(0, H1, 2 * t), (H1, P, 2 * t + 1)], None)
                        load_tile(layer, pr, PAIRS, 0, 0, base + PAIRS, [(0, H1, E1), (H1, P, E1)], None)

            def expert_records():
                gu, dp = a["L1_ffn_gu_w"], a["L1_ffn_dp_w"]
                with sp.Fori(0, PAIRS // WSLOTS) as h:
                    for u in range(WSLOTS):
                        E = WSLOTS * h + u
                        sp.wait_ge(e_turned, E + 1)
                        sp.sem_inc(past_sp, 1)
                        for q in range(2):
                            e = bass.ds(2 * E + q, 1)
                            rows = slice(q * H1, q * H1 + H1)
                            sp.dma_start(estage[rows, u, 0, :], gu[e, 0:H1, :].rearrange("e i c -> (e i) c")).then_inc(e_loaded[u], 16)
                            sp.dma_start(estage[rows, u, 1, :], gu[e, H1:2 * H1, :].rearrange("e i c -> (e i) c")).then_inc(e_loaded[u], 16)
                            sp.dma_start(estage[:, u, 2, :].rearrange("p (k r) -> p k r", k=KT)[:, :, rows],
                                         dp[e, :, :].rearrange("e (k p) r -> p (e k) r", p=P)).then_inc(e_loaded[u], 16)
                    for u in range(WSLOTS):
                        E = WSLOTS * h + u
                        sp.wait_ge(e_lo, E + 2)
                        sp.sem_inc(past_sp, 1)
                        sp.dma_start(wrec1[bass.ds(E, 1), :, :].rearrange("t p w -> (t p) w"),
                                     wslot[:, u, :, :].rearrange("p h w -> p (h w)").bitcast(F32)).then_inc(e_stored[u], 16)
                for u in range(WSLOTS):
                    sp.wait_ge(e_stored[u], 16 * (PAIRS // WSLOTS) + 16)

            def ssm():
                def move_b(b, j):
                    rows = slice(2 * NST * j, 2 * NST * (j + 1))
                    sp.dma_start(bqh[:, j, :].bitcast(F32), bh_all[rows, b, :].bitcast(F32)).then_inc(bq_in[j], 16)
                    sp.dma_start(bql[:, j, :].bitcast(F32), bl_all[rows, b, :].bitcast(F32)).then_inc(bq_in[j], 16)

                sp.wait_ge(b_lo, 1)
                for j in range(JT):
                    move_b(0, j)
                sp.wait_ge(b_lo, NBATCH)
                with sp.Fori(0, NBATCH - 1) as b:
                    for j in range(JT):
                        sp.wait_ge(bx_done, STEPS * b + NST * (j + 1) + RING)
                        sp.sem_inc(past_sp, 1)
                        move_b(b + 1, j)

            ffn(F0A)
            expert_records()
            ffn(F0B)
            ffn(F1A)
            ssm()
            ffn(F1B)
            orow = out.rearrange("b (t p) c -> p (b t) c", p=P)
            for g in range(8):
                sp.wait_ge(out_kept, g + 1)
                sp.dma_start(orow[:, 2 * g:2 * g + 2, :], outbuf[:, 2 * g:2 * g + 2, :]).then_inc(stored, 16)
            sp.wait_ge(stored, 16 * 8)

        def turned_groups():
            groups = []
            for b in range(NBATCH):
                half = (xnat if b < 2 else xnat2).rearrange("p (t c) -> p t c", c=C)
                for k in range(KT):
                    srcs = [(half[:, (NT * b + i) % 8, k * P:k * P + P], i * P) for i in range(NT)]
                    groups.append((srcs, P, [(xT[:, k, b, :], lambda v: v[:, 0:SEQ])]))
            for r in range(0, 10, 2):
                srcs = [(st_in[:, r + q, k * P:k * P + P], (2 * k + q) * P) for k in range(KT) for q in range(2)]
                whole = lambda v: v[:, 0:SEQ].rearrange("p (k n) -> p k n", k=KT)
                if r < JT:
                    copies = [(w_in[:, :, OZ + r * P:OZ + r * P + 2 * P], whole)]
                elif r == JT:
                    xrep = w_in[:, :, OX:OX + DI].rearrange("p k (h r n) -> p k h r n", h=XH, r=REP)
                    copies = [(xrep[:, k, :, q, :],
                               lambda v, k=k: v[:, 2 * k * P:2 * k * P + P].rearrange("p (h n) -> p h n", h=XH))
                              for k in range(KT) for q in range(REP)]
                    copies.append((w_in[:, :, OB:OB + DXB], lambda v: whole(v)[:, :, P:2 * P]))
                else:
                    copies = [(w_in[:, :, OC + (r - 6) * P:OC + (r - 4) * P], whole)]
                groups.append((srcs, P, copies))
            groups.append(([(st_dtin[:, k * P:k * P + P], k * P) for k in range(KT)], P,
                           [(w_dtin[:, :, :], lambda v: v[:, 0:C].rearrange("p (k n) -> p k n", k=KT))]))
            groups.append(([(st_dt[:, j, :], j * P) for j in range(JT)], P, [(w_dt[:, :], lambda v: v[:, 0:DI])]))
            for h in range(2):
                srcs = [(st_out[:, k, (2 * h + j) * P:(2 * h + j + 1) * P], (2 * j + k) * P)
                        for j in range(2) for k in range(KT)]
                groups.append((srcs, P, [(w_out[:, 2 * h:2 * h + 2, :],
                                          lambda v: v[:, 0:SEQ].rearrange("p (j n) -> p j n", j=2))]))
            for st, gw, n in ((st_g0, gw0, E0), (st_g1, gw1, R1)):
                groups.append(([(st[0:n, k * P:k * P + P], k * n) for k in range(KT)], n,
                               [(gw[:, :, :], lambda v, n=n: v[:, 0:KT * n].rearrange("p (k n) -> p k n", k=KT))]))
            return groups

        TURNED = turned_groups()
        NX = NBATCH * KT

        UNITS = []
        for h in range(0, HEADS, 2):
            UNITS += [[(3, h, 0, 4)], [(2, h, 0, 3), (0, h, 3, 1)],
                      [(3, h + 1, 0, 4)], [(2, h + 1, 0, 3), (0, h + 1, 3, 1)],
                      [(1, h, 0, 2), (1, h + 1, 2, 2)]]
        NU = len(UNITS)
        PER_PAIR = NU // EPB

        @block.gpsimd
        def _(pool):
            done = [0]

            def link(ins):
                done[0] += 1
                ins.then_inc(consts, 1)
                pool.wait_ge(consts, done[0])

            selt = arena[:, 8192:8192 + NST * P]
            selt_b = arena[:, 8192 + NST * P:8192 + 2 * NST * P]
            link(pool.memset(ident[:], 0.0))
            link(pool.affine_select(out=ident[:], in_=ident[:], compare_op=ALU.not_equal, fill=1.0, base=0,
                                    pattern=[[-1, P]], channel_multiplier=1))
            link(pool.memset(ones[:], 1.0 / C))
            link(pool.memset(zerob[:], 0.0))
            link(pool.memset(epsc[:], EPS))
            link(pool.memset(maskb[:], 0.0))
            link(pool.affine_select(out=maskb[:], in_=maskb[:], compare_op=ALU.is_ge, fill=NEG, base=0,
                                    pattern=[[-1, P]], channel_multiplier=1))
            link(pool.tensor_copy(identb[:], ident[:]))
            link(pool.memset(headmask[:], 1.0))
            link(pool.affine_select(out=headmask[:], in_=headmask[:], compare_op=ALU.is_ge, fill=0.0, base=0,
                                    pattern=[[-HD, HPT]], channel_multiplier=1))
            link(pool.affine_select(out=headmask[:], in_=headmask[:], compare_op=ALU.is_ge, fill=0.0, base=HD - 1,
                                    pattern=[[HD, HPT]], channel_multiplier=-1))
            for e in range(E0):
                link(pool.memset(iota0[:, e:e + 1], float(e)))
            link(pool.memset(selt, 0.0))
            link(pool.affine_select(out=selt.rearrange("p (n h m) -> p n h m", n=NST, h=HPT),
                                    in_=selt.rearrange("p (n h m) -> p n h m", n=NST, h=HPT),
                                    compare_op=ALU.not_equal, fill=1.0, base=0,
                                    pattern=[[1, NST], [NST, HPT], [0, NST]], channel_multiplier=-1))
            link(pool.tensor_copy(sel_c[:, :, :].rearrange("p n m -> p (n m)"), selt))
            link(pool.memset(selt_b, 0.0))
            link(pool.affine_select(out=selt_b.rearrange("p (n h m) -> p n h m", n=NST, h=2),
                                    in_=selt_b.rearrange("p (n h m) -> p n h m", n=NST, h=2),
                                    compare_op=ALU.not_equal, fill=1.0, base=0,
                                    pattern=[[1, NST], [NST, 2], [0, 64]], channel_multiplier=-1))
            link(pool.tensor_copy(sel_b[:, :, :].rearrange("p n m -> p (n m)"), selt_b[0:2 * NST, :]))
            assert done[0] == NCONST
            for g in (TILES0 - 1, NPREP - 1):
                s, r = g % WSLOTS, padding(g)
                pool.wait_ge(rec_turned, g - WSLOTS + 1)
                if g >= TILES0:
                    pool.wait_ge(padded, 2)
                pool.memset(stage[r:P, s, 0:2, :], 0.0).then_inc(padded, 1)
                pool.wait_ge(padded, 1 if g < TILES0 else 3)
                pool.memset(stage[:, s, 2, :].rearrange("p (k r) -> p k r", k=KT)[:, :, r:P], 0.0).then_inc(padded, 1)
            pool.sem_inc(weighted, RING)
            pool.sem_inc(y_added, RING)

            def weigh(q, c, r):
                pool.wait_ge(prod_done, q + 1 + RING)
                pool.wait_ge(hid_lo, q + 1)
                pool.tensor_tensor(iw[:, c, :], prod[:, c, :], wbc[:, r, c, :], ALU.mult).then_inc(weighted, 1)

            def tile(layer, pr, t, r, nth, base):
                pool.wait_ge(wbc_in[r], 32 * (ring_count(layer, pr, r) + nth + 1))
                for c in range(2):
                    weigh(2 * (base + t) + c, c, r)

            def ffn(layer):
                n = TILES[layer]
                with pool.Fori(0, PAIRS_OF) as pr:
                    base = tiles_before(layer, pr)
                    with pool.Fori(0, n // RING) as i:
                        for u in range(RING):
                            tile(layer, pr, RING * i + u, u, i, base)
                    for t in range(n // RING * RING, n):
                        tile(layer, pr, t, t % RING, t // RING, base)

            def ssm():
                with pool.Fori(0, NBATCH) as b:
                    for j in range(JT):
                        pool.wait_ge(skip_set, JT * b + j + 1)
                        for n in range(NST):
                            s = STEPS * b + NST * j + n
                            pool.wait_ge(hc_done, s + 1 + RING)
                            pool.wait_ge(y_added, s + RING)
                            pool.tensor_tensor(xact[:, j % RING, :], xact[:, j % RING, :], hc[:, n % RING, :], ALU.add).then_inc(y_added, 1)

            ffn(F0A)
            ffn(F0B)
            ffn(F1A)
            ssm()
            ffn(F1B)

        @block.tensor
        def _(pe):
            pe.wait_ge(consts, NCONST)
            for n, (srcs, rows, _) in enumerate(TURNED):
                if n == 0:
                    pe.wait_ge(x_loaded, 32)
                if n == NX:
                    pe.wait_ge(w_loaded, 16 * 7)
                if n >= RING:
                    pe.wait_ge(m_kept, n - RING + 1)
                for src, at in srcs:
                    last = pe.transpose(ps[:, 4 + n % RING, at:at + rows], src, ident[0:rows, 0:rows])
                last.then_inc(m_turned, 1)
            for g in range(NPREP):
                s, bank = g % WSLOTS, 2 * (g % RING)
                pe.wait_ge(stage_loaded[s], stage_count(g))
                if padding(g) < P:
                    pe.wait_ge(padded, 2 if g < TILES0 else 4)
                pe.wait_ge(rec_lo, g + 1)
                for w in range(2):
                    for k in range(KT):
                        pe.transpose(ps[:, bank, (2 * k + w) * P:(2 * k + w + 1) * P], stage[:, s, w, k * P:k * P + P], ident[:])
                for k in range(KT):
                    last = pe.transpose(ps[:, bank + 1, k * P:k * P + P], stage[:, s, 2, k * P:k * P + P], ident[:])
                last.then_inc(rec_turned, 1)
            pe.sem_inc(down_done, RING)
            pe.sem_inc(e_turned, WSLOTS)
            pe.sem_inc(c_spread, RING)
            pe.sem_inc(route_turned, 1)
            pe.sem_inc(prob_turned, RING)
            pe.sem_inc(pv_done, RING)

            def product(bank, pairs, start=True, stop=True):
                for n, (w, v) in enumerate(pairs):
                    last = pe.matmul(bank, w, v, start=start and n == 0, stop=stop and n == len(pairs) - 1)
                return last

            def normalise(layer, b, c, x_count):
                R = layer * NBATCH + b
                pe.wait_ge(x_updated, x_count + 1)
                product(ps[:, 4 + c, :], [(ones[:], xT[:, k, b, :]) for k in range(KT)]).then_inc(mean_ready, 1)
                return R

            def variance(R, c):
                pe.wait_ge(squared, R + 1)
                product(ps[:, 6 + c, :], [(ones[:], sq[:, c, k, :]) for k in range(KT)]).then_inc(var_ready, 1)

            def route(layer, R, c, routed):
                gw, E = (gw0, E0) if layer in (F0A, F0B) else (gw1, R1)
                pe.wait_ge(xn_ready, KT * (R + 1))
                for i in range(NT):
                    last = product(ps[:, 4 + c, i * E:i * E + E],
                                   [(xn[:, c, k, i * P:i * P + P], gw[:, k, :]) for k in range(KT)])
                last.then_inc(logits_ready, 1)

            def route_turn(layer, c, routed):
                rows = R0 if layer in (F0A, F0B) else R1
                pe.wait_ge(route_ready, routed + 2)
                for i in range(NT):
                    last = pe.transpose(ps[0:rows, 6 + c, i * P:i * P + P], wr[:, i, 0:rows], ident[:])
                last.then_inc(route_turned, 1)

            def gate_up(q, c, s):
                pe.wait_ge(silu_done, q + 1)
                for w, bank, free, ready in ((0, 4 + c, silu_done, gate_ready), (1, 6 + c, prod_done, up_ready)):
                    if w:
                        pe.wait_ge(prod_done, q + 1)
                    pairs = []
                    for k in range(KT):
                        at = slice((2 * k + w) * P, (2 * k + w + 1) * P)
                        pairs += [(wslot[:, s, 0, at], xnh[:, c, k, :]), (wslot[:, s, 0, at], xnl[:, c, k, :]),
                                  (wslot[:, s, 1, at], xnh[:, c, k, :])]
                    product(ps[:, bank, :], pairs).then_inc(ready, 1)

            def down(q, c, s):
                pe.wait_ge(hid_lo, q + 1 + RING)
                for k in range(KT):
                    at = slice(2 * KT * P + k * P, 2 * KT * P + k * P + P)
                    for w, v in ((wslot[:, s, 0, at], iwh[:, c, :]), (wslot[:, s, 0, at], iwl[:, c, :]),
                                 (wslot[:, s, 1, at], iwh[:, c, :])):
                        last = pe.matmul(ps[:, 2 * c + k, :], w, v, start=False, stop=False, skip_group_check=True)
                last.then_inc(down_done, 1)

            def ffn(layer):
                n = TILES[layer]
                with pe.Fori(0, PAIRS_OF) as pr:
                    base = tiles_before(layer, pr)
                    Rs = [normalise(layer, 2 * pr + c, c, x_before(layer)) for c in range(2)]
                    for c in range(2):
                        variance(Rs[c], c)
                    for c in range(2):
                        route(layer, Rs[c], c, None)
                    for c in range(2):
                        route_turn(layer, c, ROUTED[layer] * NBATCH + 2 * pr + c)
                    pe.wait_ge(x_updated, x_before(layer) + 2 * KT * pr + 1)
                    for k in range(2 * KT):
                        pe.matmul(ps[:, k, :], zerob[:, 0:P], zerob[:], start=True, stop=False, skip_group_check=True)
                    pe.wait_ge(xn_lo, ROUTED[layer] * NBATCH + 2 * pr + 2)
                    pe.wait_ge(route_kept, ROUTED[layer] * NBATCH + 2 * pr + 2)

                    def first(t, s, nth):
                        pe.wait_ge(wrec_in[s], 16 * (slot_count(layer, pr, s) + nth + 1))
                        for c in range(2):
                            gate_up(2 * (base + t) + c, c, s)

                    def both(t, s, sprev, nth):
                        pe.wait_ge(wrec_in[s], 16 * (slot_count(layer, pr, s) + nth + 1))
                        for c in range(2):
                            down(2 * (base + t) - 2 + c, c, sprev)
                            gate_up(2 * (base + t) + c, c, s)

                    first(0, 0, 0)
                    turns = (n - 1) // WSLOTS
                    with pe.Fori(0, turns) as i:
                        for u in range(WSLOTS):
                            s = (u + 1) % WSLOTS
                            both(WSLOTS * i + u + 1, s, u, i + (u + 1) // WSLOTS)
                    for t in range(turns * WSLOTS + 1, n):
                        both(t, t % WSLOTS, (t - 1) % WSLOTS, t // WSLOTS)
                    for c in range(2):
                        down(2 * (base + n) - 2 + c, c, (n - 1) % WSLOTS)
                    for k in range(2 * KT):
                        last = pe.matmul(ps[:, k, :], zerob[:, 0:P], zerob[:], start=False, stop=True, skip_group_check=True)
                    last.then_inc(ffn_out, 1)

            def attention():
                with pe.Fori(0, NBATCH) as b:
                    R = normalise(ATT, b, 0, x_before(ATT) + KT * b)
                    variance(R, 0)
                    pe.wait_ge(xn_ready, KT * (R + 1))
                    pe.wait_ge(e_lo, EPB * b + 1)
                    for m in range(KT):
                        product(ps[:, m, :], [(wq[:, k, m * P:m * P + P], xn[:, 0, k, :]) for k in range(KT)]).then_inc(qkv_ready, 1)
                    product(ps[:, 2, :], [(wk[:, k, :, :].rearrange("p m d -> p (m d)"), xn[:, 0, k, :]) for k in range(KT)]).then_inc(qkv_ready, 1)
                    for i in range(NT):
                        last = product(ps[:, 3, i * HD:i * HD + HD],
                                       [(xn[:, 0, k, i * P:i * P + P], wv[:, k, :]) for k in range(KT)])
                    last.then_inc(qkv_ready, 1)
                    pe.wait_ge(q_kept, KT * (b + 1))
                    pe.wait_ge(k_kept, HPT * (b + 1))
                    pe.wait_ge(v_kept, b + 1)

                    def scores(u):
                        U = NU * b + u
                        pe.wait_ge(prob_ready, U + 1)
                        for i, h, at, n in UNITS[u]:
                            pe.matmul(ps[:, 4 + u % RING, at * P:(at + n) * P], qT[:, h // HPT, i * P:i * P + P],
                                      kpad[:, h % HPT, 0:n * P], start=True, stop=False)
                            last = pe.matmul(ps[:, 4 + u % RING, (at + n - 1) * P:(at + n) * P], identb[:], maskb[:],
                                             start=False, stop=True)
                        last.then_inc(score_ready, 1)

                    def turn(u):
                        U = NU * b + u
                        pe.wait_ge(prob_ready, U + 1 + RING)
                        pe.wait_ge(probT_kept, U + 1)
                        for m in range(NT):
                            last = pe.transpose(ps[:, 6 + u % RING, m * P:m * P + P], prob[:, u % RING, m * P:m * P + P], ident[:])
                        last.then_inc(prob_turned, 1)

                    def values(u):
                        U = NU * b + u
                        pe.wait_ge(probT_kept, U + 1 + RING)
                        for i, h, at, n in UNITS[u]:
                            col = (i % 2) * C + h * HD
                            last = product(ps[:, 2 + i // 2, col:col + HD],
                                           [(probT[:, u % RING, (at + m) * P:(at + m + 1) * P], vt[:, m, :]) for m in range(n)])
                        last.then_inc(pv_done, 1)

                    def turn_experts(i):
                        s = i % WSLOTS
                        pe.wait_ge(e_loaded[s], 96 * (EPB // WSLOTS * b + i // WSLOTS) + 96)
                        pe.wait_ge(e_lo, EPB * b + i + 1)
                        for w in range(2):
                            for k in range(KT):
                                pe.transpose(ps[:, 0, (2 * k + w) * P:(2 * k + w + 1) * P], estage[:, s, w, k * P:k * P + P], ident[:])
                        for k in range(KT):
                            last = pe.transpose(ps[:, 1, k * P:k * P + P], estage[:, s, 2, k * P:k * P + P], ident[:])
                        last.then_inc(e_turned, 1)

                    for u in range(NU + 2):
                        if u < NU:
                            scores(u)
                        if u < NU and u % PER_PAIR == 1:
                            turn_experts(u // PER_PAIR)
                        if 1 <= u <= NU:
                            turn(u - 1)
                        if u >= 2:
                            values(u - 2)
                    pe.wait_ge(o_normed, 2 * (b + 1))
                    for m in range(KT):
                        for i in range(NT):
                            last = pe.transpose(ps[:, 4 + m, i * P:i * P + P], osb[:, i, m * P:m * P + P], ident[:])
                        last.then_inc(o_turned, 1)
                    pe.wait_ge(o_kept, KT * (b + 1))
                    for k in range(KT):
                        last = product(ps[:, 6 + k, :], [(wo[:, m, k * P:k * P + P], oT[:, m, :]) for m in range(KT)])
                    last.then_inc(attn_out, 1)

            def ssm():
                for b in range(0, NBATCH, 2):
                    if b:
                        pe.wait_ge(centred, KT * (SSM * NBATCH + b))
                    Rs = [normalise(SSM, b + c, c, x_before(SSM)) for c in range(2)]
                    if b:
                        pe.wait_ge(log_done, SSM * NBATCH + b)
                    for c in range(2):
                        variance(Rs[c], c)
                for b in range(NBATCH):
                    if b >= 2:
                        pe.wait_ge(b_lo, b - 1)
                        pe.wait_ge(dt_in_kept, b - 1)
                    pe.wait_ge(xn_ready, KT * (SSM * NBATCH + b + 1))
                    product(ps[:, (2 * b) % 4, :], [(w_in[:, k, OB:OB + P], xns[:, b, k, :]) for k in range(KT)]).then_inc(b_ready, 1)
                    product(ps[:, (2 * b + 1) % 4, :], [(w_dtin[:, k, :], xns[:, b, k, :]) for k in range(KT)]).then_inc(dt_in_ready, 1)

                def project(N, m, b, j):
                    pe.wait_ge(proj_taken, JOBS * N + m + 1)
                    if m == 2:
                        pe.wait_ge(dt_in_kept, NBATCH)
                    if m == 3:
                        pe.wait_ge(c_lo, N + 1)
                    pe.sem_inc(past_pe, 1)
                    if m == 2:
                        pairs = [(w_dt[:, j * P:(j + 1) * P], dt_in[:, b, :])]
                    else:
                        at = {0: OX, 1: OC, 3: OZ}[m] + j * P
                        pairs = [(w_in[:, k, at:at + P], xns[:, b, k, :]) for k in range(KT)]
                    product(ps[:, 4 + m % 2, :], pairs).then_inc(proj_ready, 1)

                def put_out(J, j):
                    pe.wait_ge(y_gated, J + 2)
                    pe.wait_ge(x_updated, x_before(SSM) + KT * J + 1)
                    for k in range(KT):
                        pe.matmul(ps[:, 6 + k, :], w_out[:, j, k * P:k * P + P], xact[:, j % RING, :]).then_inc(y_out, 1)

                pe.wait_ge(centred, KT * NBATCH * (SSM + 1))
                pe.wait_ge(log_done, NBATCH * (SSM + 1))
                for m in range(JOBS):
                    project(0, m, 0, 0)
                pe.wait_ge(b_lo, NBATCH)
                with pe.Fori(0, NBATCH) as b:
                    after = (b + 1) % NBATCH
                    for j in range(JT):
                        J = JT * b + j
                        ahead = (J + 1, b, j + 1) if j < JT - 1 else (J + 1, after, 0)

                        def job(m):
                            project(ahead[0], m, ahead[1], ahead[2])

                        pe.wait_ge(bq_in[j], 32 * b + 32)
                        pe.wait_ge(c_lo, J + 1)
                        for n in range(NST):
                            s = STEPS * b + NST * j + n
                            pe.wait_ge(bx_done, s + 1)
                            product(ps[:, n % RING, :], [(sel_b[:, n, :], bqh[:, j, :]), (sel_b[:, n, :], bql[:, j, :])]).then_inc(b_spread, 1)
                            pe.wait_ge(hc_done, s + 1)
                            product(ps[:, 2 + n % RING, :], [(sel_c[:, n, :], iwh[:, j % RING, :]), (sel_c[:, n, :], iwl[:, j % RING, :])]).then_inc(c_spread, 1)
                            if n in (0, 3, 5, 7):
                                job((0, 3, 5, 7).index(n))
                            if n == 2 and j:
                                put_out(J - 1, j - 1)
                    put_out(JT * b + JT - 1, JT - 1)

            pe.wait_ge(small_ready, 3)
            pe.wait_ge(m_kept, len(TURNED))
            pe.wait_ge(rec_lo, NPREP + RING)
            pe.wait_ge(small_loaded, 160)
            ffn(F0A)
            attention()
            ffn(F0B)
            ffn(F1A)
            ssm()
            ffn(F1B)
            pe.wait_ge(x_updated, x_before(6) + 1)
            for g in range(8):
                if g >= RING:
                    pe.wait_ge(out_kept, g - RING + 1)
                for i in range(2):
                    t = 2 * g + i
                    for k in range(KT):
                        last = pe.transpose(ps[:, g % RING, i * C + k * P:i * C + k * P + P],
                                            xT[:, k, t // NT, (t % NT) * P:(t % NT + 1) * P], ident[:])
                last.then_inc(out_turned, 1)

        @block.scalar
        def _(act):
            with nc.allow_non_contiguous_dma(reason="columns of 512 parameters, once"):
                act.dma_start(bias0[:], a["L0_ffn_gate_bias"].rearrange("(o e) -> o e", o=1).broadcast_to([P, E0])).then_inc(small_loaded, 16)
                act.dma_start(conv_w[:], a["L1_attn_conv_w"].rearrange("(j p) k -> p j k", p=P)).then_inc(small_loaded, 16)
                act.dma_start(conv_b[:], a["L1_attn_conv_b"].rearrange("(j p) -> p j", p=P)).then_inc(small_loaded, 16)
                act.dma_start(dt_b[:], a["L1_attn_dt_proj_b"].rearrange("(j p) -> p j", p=P)).then_inc(small_loaded, 16)
                act.dma_start(d_skip[:], a["L1_attn_D"].rearrange("(j p) -> p j", p=P)).then_inc(small_loaded, 16)
                act.dma_start(a_neg[:], a["L1_attn_A_log"].rearrange("(j p) n -> p j n", p=P)).then_inc(small_loaded, 16)
                act.dma_start(wq[:], a["L0_attn_Wq"].rearrange("(k p) n -> p k n", p=P)).then_inc(small_loaded, 16)
                act.dma_start(wo[:], a["L0_attn_Wo"].rearrange("(k p) n -> p k n", p=P)).then_inc(small_loaded, 16)
                act.dma_start(wk[:, :, 0, :], a["L0_attn_Wk"].rearrange("(k p) n -> p k n", p=P)).then_inc(small_loaded, 16)
                act.dma_start(wv[:], a["L0_attn_Wv"].rearrange("(k p) n -> p k n", p=P)).then_inc(small_loaded, 16)
            act.wait_ge(small_loaded, 160)
            act.activation(a_neg[:], a_neg[:], ACT.Exp).then_inc(a_ready, 1)
            for g in range(NPREP):
                s, bank = g % WSLOTS, 2 * (g % RING)
                act.wait_ge(rec_turned, g + 1)
                if g >= WSLOTS:
                    act.wait_ge(rec_stored[s], 16 * (g // WSLOTS))
                act.activation(wslot[:, s, 0, :], ps[:, bank:bank + 2, :].rearrange("p k s -> p (k s)")[:, 0:REC],
                               ACT.Copy).then_inc(rec_hi, 1)
            act.sem_inc(silu_done, RING)
            act.sem_inc(proj_taken, RING)
            act.sem_inc(prob_ready, RING)

            def spread(layer, b, cs, into=None):
                R = [layer * NBATCH + b + c for c in cs]
                for c in cs:
                    act.wait_ge(centred, KT * (R[c] + 1))
                    act.activation(sq[:, c, :, :], xn[:, c, :, :] if into is None else into[c], ACT.Square).then_inc(squared, 1)
                for c in cs:
                    act.wait_ge(var_ready, R[c] + 1)
                    act.activation(sq[:, c, 0, :], ps[:, 6 + c, :], ACT.Ln, bias=epsc[:, 0:1]).then_inc(log_done, 1)
                for c in cs:
                    act.wait_ge(log_done, R[c] + 1)
                    act.activation(sq[:, c, 0, :], sq[:, c, 0, :], ACT.Exp, scale=-0.5).then_inc(rstd_ready, 1)
                return R

            def silu(q, c):
                act.wait_ge(gate_ready, q + 1)
                act.wait_ge(prod_done, q + 1)
                act.activation(gact[:, c, :], ps[:, 4 + c, :], ACT.Silu).then_inc(silu_done, 1)

            def hidden_hi(q, c):
                act.wait_ge(weighted, q + 1 + RING)
                act.wait_ge(down_done, q + 1)
                act.activation(iwh[:, c, :], iw[:, c, :], ACT.Copy).then_inc(hid_hi, 1)

            def ffn(layer):
                n = TILES[layer]
                with act.Fori(0, PAIRS_OF) as pr:
                    base = tiles_before(layer, pr)
                    R = spread(layer, 2 * pr, (0, 1))
                    for c in range(2):
                        act.wait_ge(xn_ready, KT * (R[c] + 1))
                        act.activation(xnh[:, c, :, :], xn[:, c, :, :], ACT.Copy).then_inc(xn_hi, 1)
                    for c in range(2):
                        routed = ROUTED[layer] * NBATCH + 2 * pr + c
                        if layer in (F0A, F0B):
                            act.wait_ge(logits_ready, routed + 1)
                            act.wait_ge(route_ready, routed + 1)
                            act.activation(ex[:, :, 0:E0], ps[:, 4 + c, 0:NT * E0].rearrange("p (i e) -> p i e", i=NT),
                                           ACT.Exp, scale=-1.0).then_inc(route_exp, 1)
                        else:
                            act.wait_ge(route_dve, dve_route_before(layer, 2 * pr + c) + 11)
                            act.activation(ex[:, :, 0:E1], ex[:, :, 0:E1], ACT.Exp)
                            act.activation(ex[:, :, E1:R1], lg[:, :, E1:R1], ACT.Exp, scale=-1.0).then_inc(route_exp, 1)
                    for c in range(2):
                        routed = ROUTED[layer] * NBATCH + 2 * pr + c
                        rows = R0 if layer in (F0A, F0B) else R1
                        act.wait_ge(route_turned, routed + 2)
                        act.wait_ge(route_stored, 16 * routed + 16)
                        act.activation(wts[c][0:rows, :], ps[0:rows, 6 + c, :], ACT.Copy).then_inc(route_kept, 1)
                    act.activation(tiny[:, 0:1], epsc[:, 0:1], ACT.Silu)
                    with act.Fori(0, n) as t:
                        for c in range(2):
                            silu(2 * (base + t) + c, c)
                            hidden_hi(2 * (base + t) + c, c)

            def attention():
                with act.Fori(0, NBATCH) as b:
                    spread(ATT, b, (0,))
                    for m in range(KT):
                        act.wait_ge(qkv_ready, 4 * b + m + 1)
                        act.activation(qT[:, m, :], ps[:, m, :], ACT.Copy).then_inc(q_kept, 1)
                    act.wait_ge(qkv_ready, 4 * (b + 1))
                    act.activation(vt[:, :, :], ps[:, 3, 0:NT * HD].rearrange("p (i d) -> p i d", i=NT), ACT.Copy).then_inc(v_kept, 1)
                    act.wait_ge(inv_ready, b + 1)
                    for u in range(NU):
                        U, r = NU * b + u, u % RING
                        act.wait_ge(negmax, U + 1)
                        act.wait_ge(prob_turned, U + 1)
                        for p, (i, h, at, n) in enumerate(UNITS[u]):
                            last = act.activation(prob[:, r, at * P:(at + n) * P], ps[:, 4 + r, at * P:(at + n) * P], ACT.Exp,
                                                  bias=nb[:, r, p:p + 1], scale=SCALE, accum_out=psums[:, i, h:h + 1])
                        last.then_inc(prob_ready, 1)
                        if u % PER_PAIR == 2:
                            i = u // PER_PAIR
                            act.wait_ge(e_turned, EPB * b + i + 1 + WSLOTS)
                            act.wait_ge(e_stored[i % WSLOTS], 16 * (EPB // WSLOTS * b + i // WSLOTS) + 16)
                            act.activation(wslot[:, i % WSLOTS, 0, :], ps[:, 0:2, :].rearrange("p k s -> p (k s)")[:, 0:REC],
                                           ACT.Copy).then_inc(e_hi, 1)
                    for m in range(KT):
                        act.wait_ge(o_turned, KT * b + m + 1)
                        act.activation(oT[:, m, :], ps[:, 4 + m, :], ACT.Copy).then_inc(o_kept, 1)

            def ssm():
                for b in range(0, NBATCH, 2):
                    if b:
                        act.wait_ge(xn_ready, KT * (SSM * NBATCH + b))
                    spread(SSM, b, (0, 1), [xns[:, b + c, :, :] for c in range(2)])
                for b in range(NBATCH):
                    act.wait_ge(b_ready, b + 1)
                    act.activation(bh_all[:, b, :], ps[:, (2 * b) % 4, :], ACT.Copy).then_inc(b_hi, 1)
                    act.wait_ge(dt_in_ready, b + 1)
                    act.activation(dt_in[:, b, :], ps[:, (2 * b + 1) % 4, :], ACT.Copy).then_inc(dt_in_kept, 1)

                def take(N, m, r, j, ring):
                    act.wait_ge(proj_ready, JOBS * N + m + 1)
                    if m == 0:
                        if ring:
                            act.wait_ge(bx_done, NST * (N - 1) + RING)
                        act.activation(xpad[:, r, TAPS - 1:XPAD], ps[:, 4, :], ACT.Copy).then_inc(proj_taken, 1)
                    elif m == 1:
                        if ring:
                            act.wait_ge(c_spread, NST * (N - 1) + RING)
                        act.activation(iwh[:, r, :], ps[:, 5, :], ACT.Copy).then_inc(proj_taken, 1)
                    elif m == 2:
                        act.activation(dt[:, r, :], ps[:, 4, :], ACT.Identity, bias=dt_b[:, j:j + 1]).then_inc(proj_taken, 1)
                    else:
                        if ring:
                            act.wait_ge(y_gated, N)
                        act.activation(zg[:, r, :], ps[:, 5, :], ACT.Silu).then_inc(proj_taken, 1)

                def exp_abs(N, r, ring):
                    act.wait_ge(proj_taken, JOBS * N + 3 + RING)
                    if ring:
                        act.wait_ge(dt_done, N)
                    act.activation(sp_e, dt[:, r, :], ACT.Abs).then_inc(dt_abs, 1)
                    act.wait_ge(dt_abs, N + 1)
                    act.activation(sp_e, sp_e, ACT.Exp, scale=-1.0).then_inc(dt_exp, 1)

                def log_one(N):
                    act.wait_ge(dt_one, N + 1)
                    act.activation(sp_l, sp_1, ACT.Ln).then_inc(dt_log, 1)

                def silu_conv(N, r, j):
                    act.wait_ge(conv_done, N + 1)
                    act.activation(xact[:, r, :], xact[:, r, :], ACT.Silu, bias=conv_b[:, j:j + 1]).then_inc(conv_act, 1)

                for m in range(3):
                    take(0, m, 0, 0, False)
                exp_abs(0, 0, False)
                log_one(0)
                take(0, 3, 0, 0, False)
                silu_conv(0, 0, 0)
                act.activation(tiny[:, 1:2], epsc[:, 0:1], ACT.Exp)
                with act.Fori(0, NBATCH) as b:
                    for j in range(JT):
                        J, r = JT * b + j, j % RING
                        N, rn, jn = J + 1, (j + 1) % RING, (j + 1) % JT
                        act.wait_ge(dt_done, J + 1)
                        for n in range(NST):
                            s = STEPS * b + NST * j + n
                            act.wait_ge(scanned, s + 1)
                            act.activation(da[:, n % DECAYS, :], dt[:, r, :], ACT.Exp, scale=a_neg[:, j, n:n + 1]).then_inc(decay_ready, 1)
                            if n == 3:
                                take(N, 0, rn, jn, True)
                            if n == 5:
                                take(N, 1, rn, jn, True)
                            if n == 7:
                                take(N, 2, rn, jn, True)
                                exp_abs(N, rn, True)
                            if n == 11:
                                log_one(N)
                            if n == 13:
                                take(N, 3, rn, jn, True)
                                silu_conv(N, rn, jn)

            ffn(F0A)
            attention()
            ffn(F0B)
            ffn(F1A)
            ssm()
            ffn(F1B)

        @block.vector
        def _(dve):
            dve.sem_inc(rec_lo, RING)
            dve.sem_inc(e_lo, 1)
            dve.sem_inc(x_updated, 1)
            dve.sem_inc(prod_done, RING)
            dve.sem_inc(hid_lo, RING)
            dve.sem_inc(probT_kept, RING)
            dve.sem_inc(inv_ready, 1)
            dve.sem_inc(y_gated, 1)
            dve.sem_inc(route_ready, 1)
            dve.sem_inc(bx_done, RING)
            dve.sem_inc(hc_done, RING)
            dve.sem_inc(scanned, DECAYS)
            dve.wait_ge(small_loaded, 160)
            for k in range(KT):
                dve.tensor_copy(wk[:, k, 1:HPT, :], wk[:, k, 0:1, :].broadcast_to([P, HPT - 1, HD])).then_inc(small_ready, 1)
            dve.wait_ge(a_ready, 1)
            dve.tensor_scalar(a_neg[:], a_neg[:], -1.0, None, ALU.mult).then_inc(small_ready, 1)
            for n, (_, rows, copies) in enumerate(TURNED):
                dve.wait_ge(m_turned, n + 1)
                for dst, view in copies:
                    last = dve.tensor_copy(dst, view(ps[:, 4 + n % RING, :]))
                last.then_inc(m_kept, 1)
            for g in range(NPREP):
                s, bank = g % WSLOTS, 2 * (g % RING)
                dve.wait_ge(rec_hi, g + 1)
                dve.tensor_tensor(wslot[:, s, 1, :], ps[:, bank:bank + 2, :].rearrange("p k s -> p (k s)")[:, 0:REC],
                                  wslot[:, s, 0, :], ALU.subtract).then_inc(rec_lo, 1)

            def normalise(layer, b, cs, into=None):
                R = [layer * NBATCH + b + c for c in cs]
                for c in cs:
                    dve.wait_ge(mean_ready, R[c] + 1)
                    for k in range(KT):
                        v = xn[:, c, k, :] if into is None else into[c][:, k, :]
                        dve.tensor_tensor(v, xT[:, k, b + c, :], ps[:, 4 + c, :], ALU.subtract).then_inc(centred, 1)
                for c in cs:
                    dve.wait_ge(rstd_ready, R[c] + 1)
                    for k in range(KT):
                        v = xn[:, c, k, :] if into is None else into[c][:, k, :]
                        dve.tensor_tensor(v, v, sq[:, c, 0, :], ALU.mult).then_inc(xn_ready, 1)

            def route(layer, chunk, c):
                routed = ROUTED[layer] * NBATCH + chunk
                start = dve_route_before(layer, chunk)
                done = [0]

                def link(ins):
                    done[0] += 1
                    ins.then_inc(route_dve, 1)
                    return ins

                def after():
                    dve.wait_ge(route_dve, start + done[0])

                dve.wait_ge(logits_ready, routed + 1)
                if layer in (F0A, F0B):
                    E = E0
                    dve.wait_ge(route_exp, ROUTED_EXP(layer, chunk) + 1)
                    link(dve.tensor_scalar(ex[:, :, 0:E], ex[:, :, 0:E], 1.0, None, ALU.add))
                    after()
                    link(dve.reciprocal(lg[:, :, 0:E], ex[:, :, 0:E]))
                    after()
                    link(dve.tensor_tensor(mk[:, :, 0:E], lg[:, :, 0:E], bias0[:, :].unsqueeze(1).broadcast_to([P, NT, E]), ALU.add))
                    after()
                    dve.sem_inc(past_dve, 1)
                    for i in range(NT):
                        link(dve.max(m8[:, i, :], mk[:, i, 0:E]))
                    after()
                    dve.sem_inc(past_dve, 1)
                    for i in range(NT):
                        link(dve.max_index(ix[:, i, :], m8[:, i, :], mk[:, i, 0:E]))
                    after()
                    link(dve.tensor_copy(ixf[:, :, :], ix[:, :, 0:TOP0]))
                    after()
                    io = iota0[:, :].unsqueeze(1).broadcast_to([P, NT, E])
                    link(dve.tensor_tensor(ex[:, :, 0:E], io, ixf[:, :, 0:1].broadcast_to([P, NT, E]), ALU.is_equal))
                    link(dve.tensor_tensor(mk[:, :, 0:E], io, ixf[:, :, 1:2].broadcast_to([P, NT, E]), ALU.is_equal))
                    after()
                    link(dve.tensor_tensor(ex[:, :, 0:E], ex[:, :, 0:E], mk[:, :, 0:E], ALU.add))
                    after()
                    link(dve.tensor_tensor(ex[:, :, 0:E], ex[:, :, 0:E], lg[:, :, 0:E], ALU.mult))
                    after()
                else:
                    E = E1
                    link(dve.tensor_copy(lg[:, :, :], ps[:, 4 + c, 0:NT * R1].rearrange("p (i e) -> p i e", i=NT)))
                    after()
                    dve.sem_inc(past_dve, 1)
                    for i in range(NT):
                        link(dve.max(m8[:, i, :], lg[:, i, 0:E]))
                    after()
                    dve.sem_inc(past_dve, 1)
                    for i in range(NT):
                        link(dve.match_replace(mk[:, i, 0:E], m8[:, i, :], lg[:, i, 0:E], TAKEN))
                    after()
                    link(dve.tensor_tensor(mk[:, :, 0:E], mk[:, :, 0:E], lg[:, :, 0:E], ALU.not_equal))
                    link(dve.tensor_tensor(ex[:, :, 0:E], lg[:, :, 0:E], m8[:, :, 0:1].broadcast_to([P, NT, E]), ALU.subtract))
                    after()
                    dve.wait_ge(route_exp, ROUTED_EXP(layer, chunk) + 1)
                    link(dve.tensor_tensor(ex[:, :, 0:E], ex[:, :, 0:E], mk[:, :, 0:E], ALU.mult))
                    link(dve.tensor_scalar(ex[:, :, E:R1], ex[:, :, E:R1], 1.0, None, ALU.add))
                    after()
                link(dve.tensor_reduce(rsum[:, :], ex[:, :, 0:E], AX.X, ALU.add))
                after()
                link(dve.reciprocal(rsum[:, :], rsum[:, :]))
                after()
                dve.wait_ge(route_turned, routed + 1)
                if layer in (F0A, F0B):
                    dve.memset(wr[:, :, E:E + 1], 1.0)
                else:
                    dve.reciprocal(wr[:, :, E:E + 1], ex[:, :, E:R1])
                dve.tensor_tensor(wr[:, :, 0:E], ex[:, :, 0:E], rsum[:, :].unsqueeze(2).broadcast_to([P, NT, E]),
                                  ALU.mult).then_inc(route_ready, 1)
                assert done[0] == (D0 if layer in (F0A, F0B) else D1), done

            def multiply(q, c):
                dve.wait_ge(up_ready, q + 1)
                dve.wait_ge(silu_done, q + 1 + RING)
                dve.wait_ge(weighted, q + 1)
                dve.tensor_tensor(prod[:, c, :], gact[:, c, :], ps[:, 6 + c, :], ALU.mult).then_inc(prod_done, 1)

            def hidden_lo(q, c):
                dve.wait_ge(hid_hi, q + 1)
                dve.wait_ge(down_done, q + 1)
                dve.tensor_tensor(iwl[:, c, :], iw[:, c, :], iwh[:, c, :], ALU.subtract).then_inc(hid_lo, 1)

            def ffn(layer):
                n = TILES[layer]
                with dve.Fori(0, PAIRS_OF) as pr:
                    base = tiles_before(layer, pr)
                    normalise(layer, 2 * pr, (0, 1))
                    for c in range(2):
                        dve.wait_ge(xn_hi, ROUTED[layer] * NBATCH + 2 * pr + c + 1)
                        dve.tensor_tensor(xnl[:, c, :, :], xn[:, c, :, :], xnh[:, c, :, :], ALU.subtract).then_inc(xn_lo, 1)
                    for c in range(2):
                        route(layer, 2 * pr + c, c)
                    with dve.Fori(0, n) as t:
                        for c in range(2):
                            multiply(2 * (base + t) + c, c)
                            hidden_lo(2 * (base + t) + c, c)
                    dve.wait_ge(ffn_out, PAIRS_OF * ROUTED[layer] + pr + 1)
                    for c in range(2):
                        for k in range(KT):
                            x = xT[:, k, 2 * pr + c, :]
                            dve.scalar_tensor_tensor(x, ps[:, 2 * c + k, :], 0.5, x, ALU.mult, ALU.add).then_inc(x_updated, 1)

            def attention():
                with dve.Fori(0, NBATCH) as b:
                    normalise(ATT, b, (0,))
                    dve.wait_ge(qkv_ready, 4 * b + 3)
                    for m in range(HPT):
                        dve.tensor_scalar(kpad[:, m, :], ps[:, 2, :], headmask[:, m:m + 1], None, ALU.mult).then_inc(k_kept, 1)
                    for u in range(NU + 1):
                        U, r = NU * b + u, u % RING
                        if u < NU:
                            dve.wait_ge(score_ready, U + 1)
                            S = ps[:, 4 + r, :]
                            if len(UNITS[u]) == 1:
                                last = dve.tensor_reduce(mx[:, r, 0:1], S, AX.X, ALU.max)
                                np_ = 1
                            elif UNITS[u][1][3] == 2:
                                last = dve.tensor_reduce(mx[:, r, :], S.rearrange("p (h k) -> p h k", h=2), AX.X, ALU.max)
                                np_ = 2
                            else:
                                dve.tensor_reduce(mx[:, r, 0:1], S[:, 0:3 * P], AX.X, ALU.max)
                                last = dve.tensor_reduce(mx[:, r, 1:2], S[:, 3 * P:SEQ], AX.X, ALU.max)
                                np_ = 2
                            last.then_inc(max_found, 1)
                            dve.wait_ge(max_found, U + 1)
                            dve.wait_ge(prob_ready, U + 1)
                            dve.tensor_scalar(nb[:, r, 0:np_], mx[:, r, 0:np_], -SCALE, None, ALU.mult).then_inc(negmax, 1)
                        if u >= 1:
                            v, rv = U - 1, (u - 1) % RING
                            dve.wait_ge(prob_turned, v + 1 + RING)
                            dve.wait_ge(pv_done, v + 1)
                            dve.tensor_copy(probT[:, rv, :], ps[:, 6 + rv, :]).then_inc(probT_kept, 1)
                        if u < NU and u % PER_PAIR == 3:
                            i = u // PER_PAIR
                            dve.wait_ge(e_hi, EPB * b + i + 1)
                            dve.tensor_tensor(wslot[:, i % WSLOTS, 1, :], ps[:, 0:2, :].rearrange("p k s -> p (k s)")[:, 0:REC],
                                              wslot[:, i % WSLOTS, 0, :], ALU.subtract).then_inc(e_lo, 1)
                    dve.wait_ge(prob_ready, NU * (b + 1) + RING)
                    dve.reciprocal(pinv[:, :, :], psums[:, :, :]).then_inc(inv_ready, 1)
                    dve.wait_ge(pv_done, NU * (b + 1) + RING)
                    dve.wait_ge(inv_ready, b + 2)
                    for m in range(2):
                        dve.tensor_tensor(osb[:, 2 * m:2 * m + 2, :].rearrange("p i (h d) -> p (i h) d", d=HD),
                                          ps[:, 2 + m, :].rearrange("p (g d) -> p g d", d=HD),
                                          pinv[:, 2 * m:2 * m + 2, :].rearrange("p i h -> p (i h)").unsqueeze(2).broadcast_to([P, 2 * HEADS, HD]),
                                          ALU.mult).then_inc(o_normed, 1)
                    dve.wait_ge(attn_out, b + 1)
                    for k in range(KT):
                        x = xT[:, k, b, :]
                        dve.tensor_tensor(x, ps[:, 6 + k, :], x, ALU.add).then_inc(x_updated, 1)

            def ssm():
                dve.memset(xpad[:, :, 0:TAPS - 1], 0.0)
                for b in range(0, NBATCH, 2):
                    normalise(SSM, b, (0, 1), [xns[:, b + c, :, :] for c in range(2)])
                for b in range(NBATCH):
                    dve.wait_ge(b_hi, b + 1)
                    dve.tensor_tensor(bl_all[:, b, :], ps[:, (2 * b) % 4, :], bh_all[:, b, :], ALU.subtract).then_inc(b_lo, 1)

                def split_c(N, r):
                    dve.wait_ge(proj_taken, JOBS * N + 2 + RING)
                    dve.tensor_tensor(iwl[:, r, :], ps[:, 5, :], iwh[:, r, :], ALU.subtract).then_inc(c_lo, 1)

                def conv(N, r, j, k):
                    tap, w = xpad[:, r, k:k + SEQ], conv_w[:, j, k:k + 1]
                    if k == 0:
                        dve.wait_ge(proj_taken, JOBS * N + 1 + RING)
                        dve.tensor_scalar(xact[:, r, :], tap, w, None, ALU.mult).then_inc(conv_tap, 1)
                    else:
                        dve.wait_ge(conv_tap, (TAPS - 1) * N + k)
                        ins = dve.scalar_tensor_tensor(xact[:, r, :], tap, w, xact[:, r, :], ALU.mult, ALU.add)
                        ins.then_inc(conv_tap if k < TAPS - 1 else conv_done, 1)

                def one_plus(N):
                    dve.wait_ge(dt_exp, N + 1)
                    dve.tensor_scalar(sp_1, sp_e, 1.0, None, ALU.add).then_inc(dt_one, 1)
                    dve.wait_ge(dt_one, N + 1)
                    dve.scalar_tensor_tensor(sp_e, sp_1, -1.0, sp_e, ALU.add, ALU.subtract).then_inc(dt_lost, 1)

                def softplus_sum(N, r):
                    dve.wait_ge(dt_log, N + 1)
                    dve.scalar_tensor_tensor(dt[:, r, :], dt[:, r, :], 0.0, sp_l, ALU.max, ALU.add).then_inc(dt_sum, 1)

                def softplus_done(N, r):
                    dve.wait_ge(dt_sum, N + 1)
                    dve.wait_ge(dt_lost, N + 1)
                    dve.tensor_tensor(dt[:, r, :], dt[:, r, :], sp_e, ALU.subtract).then_inc(dt_done, 1)

                def times_x(N, r, j):
                    dve.wait_ge(conv_act, N + 1)
                    dve.wait_ge(dt_done, N + 1)
                    dve.tensor_tensor(dtx[:, r, :], dt[:, r, :], xact[:, r, :], ALU.mult).then_inc(dtx_done, 1)
                    dve.tensor_scalar(xact[:, r, :], xact[:, r, :], d_skip[:, j:j + 1], None, ALU.mult).then_inc(skip_set, 1)

                def gate(J, r):
                    dve.wait_ge(y_added, NST * J + NST + RING)
                    dve.tensor_tensor(xact[:, r, :], xact[:, r, :], zg[:, r, :], ALU.mult).then_inc(y_gated, 1)

                def add_out(J, b):
                    for k in range(KT):
                        x = xT[:, k, b, :]
                        dve.wait_ge(y_out, KT * J + k + 1)
                        dve.wait_ge(x_updated, x_before(SSM) + KT * J + 1)
                        dve.tensor_tensor(x, ps[:, 6 + k, :], x, ALU.add).then_inc(x_updated, 1)

                for k in range(TAPS):
                    conv(0, 0, 0, k)
                split_c(0, 0)
                one_plus(0)
                softplus_sum(0, 0)
                softplus_done(0, 0)
                times_x(0, 0, 0)
                with dve.Fori(0, NBATCH) as b:
                    for j in range(JT):
                        J, r = JT * b + j, j % RING
                        N, rn, jn = J + 1, (j + 1) % RING, (j + 1) % JT

                        def read_out(n):
                            s = STEPS * b + NST * j + n
                            dve.wait_ge(scanned, s + 1 + DECAYS)
                            dve.wait_ge(c_spread, s + 1 + RING)
                            dve.wait_ge(y_added, s + 1)
                            dve.tensor_tensor(hc[:, n % RING, :], hst[:, n % RING, :], ps[:, 2 + n % RING, :], ALU.mult).then_inc(hc_done, 1)

                        dve.wait_ge(dtx_done, J + 1)
                        for n in range(NST):
                            s, q = STEPS * b + NST * j + n, n % RING
                            dve.wait_ge(b_spread, s + 1)
                            dve.wait_ge(scanned, s - 1 + DECAYS)
                            dve.tensor_tensor(bx[:, q, :], dtx[:, r, :], ps[:, q, :], ALU.mult).then_inc(bx_done, 1)
                            if n:
                                read_out(n - 1)
                            dve.wait_ge(bx_done, s + 1 + RING)
                            dve.wait_ge(decay_ready, s + 1)
                            dve.wait_ge(hc_done, s + 1)
                            dve.tensor_tensor_scan(hst[:, q, :], da[:, n % DECAYS, :], bx[:, q, :], 0.0, ALU.mult, ALU.add).then_inc(scanned, 1)
                            if j and n == 1:
                                gate(J - 1, rn)
                            if j and n == 4:
                                add_out(J - 1, b)
                            if 5 <= n < 5 + TAPS:
                                conv(N, rn, jn, n - 5)
                            if n == 6:
                                split_c(N, rn)
                            if n == 9:
                                one_plus(N)
                            if n == 13:
                                softplus_sum(N, rn)
                            if n == 14:
                                softplus_done(N, rn)
                            if n == 15:
                                times_x(N, rn, jn)
                        read_out(NST - 1)
                    gate(JT * b + JT - 1, (JT - 1) % RING)
                    add_out(JT * b + JT - 1, b)

            ffn(F0A)
            attention()
            ffn(F0B)
            ffn(F1A)
            ssm()
            ffn(F1B)
            for g in range(8):
                dve.wait_ge(out_turned, g + 1)
                dve.tensor_copy(outbuf[:, 2 * g:2 * g + 2, :].rearrange("p t c -> p (t c)"), ps[:, g % RING, :]).then_inc(out_kept, 1)


def kernel(**inputs):
    import numpy as np
    import concourse.bacc as bacc
    from concourse.bass_utils import run_bass_kernel_spmd

    nc = bacc.Bacc("TRN2", target_bir_lowering=False, num_devices=1)
    arrays, aps = {}, {}
    for name, value in inputs.items():
        v = np.ascontiguousarray(value)
        arrays[f"in_{name}"] = v
        aps[name] = nc.dram_tensor(f"in_{name}", v.shape, mybir.dt.from_np(v.dtype), kind="ExternalInput").ap()
    out = nc.dram_tensor("out", inputs["L0_attn_x"].shape, F32, kind="ExternalOutput").ap()
    macaron_kernel(nc, aps, out)
    r = run_bass_kernel_spmd(nc, [arrays], core_ids=[0])
    return r.results[0]["out"]
```

```python
from contextlib import ExitStack

import concourse.bass as bass
from concourse import mybir

P = 128
ALU = mybir.AluOpType
ACT = mybir.ActivationFunctionType
AX = mybir.AxisListType
F32 = mybir.dt.float32
F32R = mybir.dt.float32r
BF16 = mybir.dt.bfloat16
U32 = mybir.dt.uint32

NEG = -1.0e30
TAKEN = -3.0e38
RING = 2
WSLOTS = 4
LEAD = 2
DECAYS = 4


def split_rows(tile, rows, expert_rows, experts):
    lo, hi = tile * P, tile * P + P
    cut = next((e * expert_rows for e in range(1, experts + 1) if lo < e * expert_rows < hi), lo + 64)
    return [(0, cut - lo, min(lo // expert_rows, experts)), (cut - lo, P, min(cut // expert_rows, experts))]


def macaron_kernel(nc, a, out):
    NBATCH, SEQ, C = a["L0_attn_x"].shape
    KT = C // P
    NT = SEQ // P
    T = NBATCH * SEQ
    EPS = 1e-5
    HEADS = C // a["L0_attn_Wk"].shape[1]
    HD = a["L0_attn_Wk"].shape[1]
    SCALE = float(HD) ** -0.5
    HPT = P // HD
    E0, G0ROWS, _ = a["L0_ffn_up_w"].shape
    H0 = G0ROWS // 2
    HS = a["L0_ffn_shared_dw"].shape[1]
    TOP0 = 2
    ROWS0 = E0 * H0 + HS
    TILES0 = -(-ROWS0 // P)
    E1, G1ROWS, _ = a["L1_ffn_gu_w"].shape
    H1 = G1ROWS // 2
    PAIRS = E1 // 2
    TILES1 = PAIRS + 1
    R0, R1 = E0 + 1, E1 + 1
    DI, NST = a["L1_attn_A_log"].shape
    DXB = 128
    XH = DXB // NST
    REP = DI // DXB
    JT = DI // P
    OZ, OX, OB, OC = 0, DI, 2 * DI, 2 * DI + DXB
    WIN = OC + DI
    TAPS = a["L1_attn_conv_w"].shape[1]
    REC = 2 * KT * P + C
    assert (SEQ, C, KT, NT, HD, NST, JT, REP, H1, TOP0) == (512, 256, 2, 4, 16, 16, 4, 4, 64, 2)

    with ExitStack() as ctx:
        def sb(name, shape, dt=F32):
            return ctx.enter_context(nc.sbuf_tensor(name, shape, dt))

        def sem(name):
            return ctx.enter_context(nc.semaphore(name))

        wrec0 = nc.dram_tensor("wrec0", (TILES0, P, 2 * REC), F32, kind="Internal").ap()
        wrec1 = nc.dram_tensor("wrec1", (TILES1, P, 2 * REC), F32, kind="Internal").ap()
        route_t = nc.dram_tensor("route_t", (R1, T), F32, kind="Internal").ap()

        xT = sb("xT", [P, KT, NBATCH, SEQ])
        xn = sb("xn", [P, RING, KT, SEQ])
        sq = sb("sq", [P, RING, KT, SEQ])
        xnh = sb("xnh", [P, RING, KT, SEQ], F32R)
        xnl = sb("xnl", [P, RING, KT, SEQ], F32R)
        wslot = sb("wslot", [P, WSLOTS, 2, REC], F32R)
        iwh = sb("iwh", [P, RING, SEQ], F32R)
        iwl = sb("iwl", [P, RING, SEQ], F32R)
        bqh = sb("bqh", [2 * NST, JT, SEQ], F32R)
        bql = sb("bql", [2 * NST, JT, SEQ], F32R)
        sel_b = sb("sel_b", [2 * NST, NST, P], F32R)
        sel_c = sb("sel_c", [P, NST, P], F32R)
        w_in = sb("w_in", [P, KT, WIN])
        w_dtin = sb("w_dtin", [P, KT, P])
        w_dt = sb("w_dt", [P, DI])
        w_out = sb("w_out", [P, JT, C])
        wq = sb("wq", [P, KT, C])
        wk = sb("wk", [P, KT, HPT, HD])
        wv = sb("wv", [P, KT, HD])
        wo = sb("wo", [P, KT, C])
        gw0 = sb("gw0", [P, KT, E0])
        gw1 = sb("gw1", [P, KT, R1])
        ident = sb("ident", [P, P])
        ones = sb("ones", [P, P])
        identb = sb("identb", [P, P], BF16)
        maskb = sb("maskb", [P, P], BF16)
        headmask = sb("headmask", [P, HPT])
        bias0 = sb("bias0", [P, E0])
        iota0 = sb("iota0", [P, E0])
        epsc = sb("epsc", [P, 1])
        conv_w = sb("conv_w", [P, JT, TAPS])
        conv_b = sb("conv_b", [P, JT])
        dt_b = sb("dt_b", [P, JT])
        d_skip = sb("d_skip", [P, JT])
        a_neg = sb("a_neg", [P, JT, NST])
        lg = sb("lg", [P, NT, R1])
        ex = sb("ex", [P, NT, R1])
        mk = sb("mk", [P, NT, R1])
        wr = sb("wr", [P, NT, R1])
        m8 = sb("m8", [P, NT, 8])
        ix = sb("ix", [P, NT, 8], U32)
        ixf = sb("ixf", [P, NT, TOP0])
        rsum = sb("rsum", [P, NT])
        mx = sb("mx", [P, RING, 2])
        nb = sb("nb", [P, RING, 2])
        psums = sb("psums", [P, NT, HEADS])
        pinv = sb("pinv", [P, NT, HEADS])
        vt = sb("vt", [P, NT, HD])
        tiny = sb("tiny", [P, 2])

        XPAD = SEQ + TAPS - 1
        ARENA = RING * XPAD + (NBATCH * KT + 6 * RING + DECAYS + 3) * SEQ
        arena = sb("arena", [P, ARENA])

        wts = [sq[:, c, 1, :] for c in range(RING)]

        def region(at, *dims):
            n = 1
            for d in dims:
                n *= d
            names = "abcd"[:len(dims)]
            v = arena[:, at:at + n]
            if len(dims) > 1:
                v = v.rearrange(f"p ({' '.join(names)}) -> p {' '.join(names)}",
                                **{k: d for k, d in zip(names[1:], dims[1:])})
            return v, at + n

        stage, o = region(0, WSLOTS, 3, C)
        st_in, o = region(o, 10, C)
        st_dtin, o = region(o, C)
        st_dt, o = region(o, JT, P)
        st_out, o = region(o, KT, DI)
        st_g0, o = region(o, C)
        st_g1, o = region(o, C)
        outbuf = region(0, 16, C)[0]
        xnat = xn[:, :, :, :].rearrange("p r k s -> p (r k s)")
        xnat2 = sq[:, :, :, :].rearrange("p r k s -> p (r k s)")
        qT, o = region(0, KT, SEQ)
        kpad, o = region(o, HPT, SEQ)
        prob, o = region(o, RING, SEQ)
        probT, o = region(o, RING, SEQ)
        osb, o = region(o, NT, C)
        oT, o = region(o, KT, SEQ)
        est0, o = region(o, RING, 3, C)
        att_end = o
        est1 = sq[:, :, :, :].rearrange("p r k s -> p (r k s)")[:, 0:RING * 3 * C].rearrange("p (u w c) -> p u w c", u=RING, w=3)
        estage = [est0[:, 0], est0[:, 1], est1[:, 0], est1[:, 1]]
        gact, o = region(0, RING, SEQ)
        prod, o = region(o, RING, SEQ)
        iw, o = region(o, RING, SEQ)
        wbc, o = region(o, RING, RING, SEQ)
        zg, o = region(0, RING, SEQ)
        xpad, o = region(o, RING, XPAD)
        xact, o = region(o, RING, SEQ)
        dt, o = region(o, RING, SEQ)
        sp_e, o = region(o, SEQ)
        sp_1, o = region(o, SEQ)
        sp_l, o = region(o, SEQ)
        da, o = region(o, DECAYS, SEQ)
        bx, o = region(o, RING, SEQ)
        hst, o = region(o, RING, SEQ)
        hc, o = region(o, RING, SEQ)
        assert att_end <= o
        xns, o = region(o, NBATCH, KT, SEQ)
        assert o == ARENA
        convd = sq[:, :, :, :].rearrange("p r k s -> p (r k s)").rearrange("p (g n) -> p g n", n=P)
        dtx = xpad[:, :, TAPS - 1:XPAD]
        bh_all = xnh[:, :, :, :].rearrange("p r k s -> p (r k) s")
        bl_all = xnl[:, :, :, :].rearrange("p r k s -> p (r k) s")
        dt_in = xn[:, :, :, :].rearrange("p r k s -> p (r k) s")

        ps = ctx.enter_context(nc.psum_tensor("ps", [P, 8, SEQ], F32))

        x_loaded = sem("x_loaded")
        w_loaded = sem("w_loaded")
        small_loaded = sem("small_loaded")
        consts = sem("consts")
        m_turned = sem("m_turned")
        small_ready = sem("small_ready")
        padded = sem("padded")
        attn_out = sem("attn_out")
        out_turned = sem("out_turned")
        m_kept = sem("m_kept")
        a_ready = sem("a_ready")
        stage_loaded = [sem(f"stage_loaded{i}") for i in range(WSLOTS)]
        rec_turned = sem("rec_turned")
        rec_hi = sem("rec_hi")
        rec_lo = sem("rec_lo")
        rec_stored = [sem(f"rec_stored{i}") for i in range(WSLOTS)]
        e_loaded = [sem(f"e_loaded{i}") for i in range(WSLOTS)]
        e_stored = [sem(f"e_stored{i}") for i in range(WSLOTS)]
        e_turned = sem("e_turned")
        e_hi = sem("e_hi")
        e_lo = sem("e_lo")
        mean_ready = sem("mean_ready")
        centred = sem("centred")
        squared = sem("squared")
        var_ready = sem("var_ready")
        log_done = sem("log_done")
        rstd_ready = sem("rstd_ready")
        xn_ready = sem("xn_ready")
        xn_hi = sem("xn_hi")
        xn_lo = sem("xn_lo")
        logits_ready = sem("logits_ready")
        route_dve = sem("route_dve")
        route_exp = sem("route_exp")
        route_ready = sem("route_ready")
        route_turned = sem("route_turned")
        route_kept = sem("route_kept")
        route_stored = sem("route_stored")
        wrec_in = [sem(f"wrec_in{i}") for i in range(WSLOTS)]
        wbc_in = [sem(f"wbc_in{i}") for i in range(RING)]
        gate_ready = sem("gate_ready")
        up_ready = sem("up_ready")
        silu_done = sem("silu_done")
        prod_done = sem("prod_done")
        weighted = sem("weighted")
        hid_hi = sem("hid_hi")
        hid_lo = sem("hid_lo")
        down_done = sem("down_done")
        x_updated = sem("x_updated")
        xn_copied = sem("xn_copied")
        qkv_ready = sem("qkv_ready")
        q_kept = sem("q_kept")
        k_kept = sem("k_kept")
        v_kept = sem("v_kept")
        score_ready = sem("score_ready")
        max_found = sem("max_found")
        negmax = sem("negmax")
        prob_ready = sem("prob_ready")
        prob_turned = sem("prob_turned")
        probT_kept = sem("probT_kept")
        pv_done = sem("pv_done")
        inv_ready = sem("inv_ready")
        o_normed = sem("o_normed")
        o_turned = sem("o_turned")
        o_kept = sem("o_kept")
        b_ready = sem("b_ready")
        b_hi = sem("b_hi")
        b_lo = sem("b_lo")
        dt_in_ready = sem("dt_in_ready")
        dt_in_kept = sem("dt_in_kept")
        bq_in = [sem(f"bq_in{j}") for j in range(JT)]
        proj_ready = sem("proj_ready")
        proj_taken = sem("proj_taken")
        diagonals = sem("diagonals")
        dt_abs = sem("dt_abs")
        dt_exp = sem("dt_exp")
        dt_one = sem("dt_one")
        dt_lost = sem("dt_lost")
        dt_log = sem("dt_log")
        dt_sum = sem("dt_sum")
        dt_done = sem("dt_done")
        dtx_done = sem("dtx_done")
        skip_set = sem("skip_set")
        c_lo = sem("c_lo")
        b_spread = sem("b_spread")
        c_spread = sem("c_spread")
        decay_ready = sem("decay_ready")
        bx_done = sem("bx_done")
        scanned = sem("scanned")
        hc_done = sem("hc_done")
        y_added = sem("y_added")
        y_gated = sem("y_gated")
        y_out = sem("y_out")
        stored = sem("stored")
        past_sp, past_pool, past_pe, past_dve = (sem(f"past_{e}") for e in ("sp", "pool", "pe", "dve"))
        out_kept = sem("out_kept")

        block = ctx.enter_context(nc.Block())

        F0A, ATT, F0B, F1A, SSM, F1B = range(6)
        ROUTED = {F0A: 0, F0B: 1, F1A: 2, F1B: 3}
        TILES = {F0A: TILES0, F0B: TILES0, F1A: TILES1, F1B: TILES1}
        FFNS = [F0A, F0B, F1A, F1B]
        PAIRS_OF = NBATCH // 2
        NCONST = 24
        D0 = 18
        D1 = 15

        def tiles_before(layer, pr):
            return sum(PAIRS_OF * TILES[f] for f in FFNS if f < layer) + pr * TILES[layer]

        def slot_uses(layer, s):
            return len([t for t in range(TILES[layer]) if t % WSLOTS == s])

        def slot_count(layer, pr, s):
            return sum(PAIRS_OF * slot_uses(f, s) for f in FFNS if f < layer) + pr * slot_uses(layer, s)

        def ring_uses(layer, s):
            return len([t for t in range(TILES[layer]) if t % RING == s])

        def ring_count(layer, pr, s):
            return sum(PAIRS_OF * ring_uses(f, s) for f in FFNS if f < layer) + pr * ring_uses(layer, s)

        def dve_route_before(layer, chunk):
            n = 0
            for f in FFNS:
                if f < layer:
                    n = n + NBATCH * (D0 if f in (F0A, F0B) else D1)
            return n + chunk * (D0 if layer in (F0A, F0B) else D1)

        def ROUTED_EXP(layer, chunk):
            return ROUTED[layer] * NBATCH + chunk

        def x_before(layer):
            return KT * NBATCH * layer + (KT * (NBATCH * (JT - 1) + 1) if layer > SSM else 0)

        JOBS = 5
        PROJ_BANK = (4, 5, 4, 5, 4)
        PARTS = (1, KT, TAPS, KT, KT)
        JOB_NAMES = ("dt", "x", "conv", "C", "z")
        PE_AT = {"dt": 0, "x": 1, "put": 3, "conv": 5, "C": 10, "z": 13}
        ACT_AT = {"skip": 2, "dt": 3, "x": 5, "log": 7, "conv": 12, "C": 12, "z": 15}
        POOL_AT = {"dtx": 13}
        DVE_AT = {"add": 5, "one": 6, "sum": 8, "done": 9, "C": 12}
        STEPS = JT * NST
        NPREP = TILES0 + 1
        EPB = PAIRS // NBATCH

        def weight_pieces(g):
            if g == TILES0:
                return [(0, H1, a["L1_ffn_sh_gate_w"], a["L1_ffn_sh_up_w"], a["L1_ffn_sh_down_w"])]
            found, r, end = [], g * P, min(g * P + P, ROWS0)
            up, down = a["L0_ffn_up_w"], a["L0_ffn_down_w"]
            shared, sdown = a["L0_ffn_shared_gw"], a["L0_ffn_shared_dw"]
            while r < end:
                e = min(r // H0, E0)
                i = r - e * H0
                m = min((H0 if e < E0 else HS) - i, end - r)
                if e < E0:
                    w = up[e, i:i + m, :], up[e, H0 + i:H0 + i + m, :], down[e, :, i:i + m]
                else:
                    w = shared[HS + i:HS + i + m, :], shared[i:i + m, :], sdown[:, i:i + m]
                found.append((r - g * P, r - g * P + m, *w))
                r += m
            return found

        def padding(g):
            return {TILES0 - 1: ROWS0 - P * (TILES0 - 1), NPREP - 1: H1}.get(g, P)

        def stage_count(g):
            return 48 * sum(len(weight_pieces(x)) for x in range(g % WSLOTS, g + 1, WSLOTS))


        @block.sync
        def _(sp):
            xr = a["L0_attn_x"].rearrange("b (t p) c -> p (b t) c", p=P)
            sp.dma_start(xnat[:, :].rearrange("p (t c) -> p t c", c=C), xr[:, 0:8, :]).then_inc(x_loaded, 16)
            sp.dma_start(xnat2[:, :].rearrange("p (t c) -> p t c", c=C), xr[:, 8:16, :]).then_inc(x_loaded, 16)
            sp.dma_start(st_in, a["L1_attn_in_proj_w"].rearrange("(r p) c -> p r c", p=P)).then_inc(w_loaded, 16)
            sp.dma_start(st_dtin, a["L1_attn_dt_in_proj_w"]).then_inc(w_loaded, 16)
            sp.dma_start(st_dt, a["L1_attn_dt_proj_w"].rearrange("(j p) c -> p j c", p=P)).then_inc(w_loaded, 16)
            sp.dma_start(st_out, a["L1_attn_out_proj_w"].rearrange("(k p) c -> p k c", p=P)).then_inc(w_loaded, 16)
            sp.dma_start(st_g0[0:E0, :], a["L0_ffn_gate_w"]).then_inc(w_loaded, 16)
            sp.dma_start(st_g1[0:E1, :], a["L1_ffn_gate_w"]).then_inc(w_loaded, 16)
            sp.dma_start(st_g1[E1:R1, :], a["L1_ffn_sh_gate1_w"]).then_inc(w_loaded, 16)

            def store_record(g):
                sp.wait_ge(rec_lo, g + 1 + RING)
                dst = wrec0[g] if g < TILES0 else wrec1[PAIRS]
                sp.dma_start(dst, wslot[:, g % WSLOTS, :, :].rearrange("p h w -> p (h w)").bitcast(F32)
                             ).then_inc(rec_stored[g % WSLOTS], 16)

            for g in range(NPREP):
                s = g % WSLOTS
                if g >= WSLOTS:
                    sp.wait_ge(rec_turned, g - WSLOTS + 1)
                for first, end, gate, up, down in weight_pieces(g):
                    dst = stage[:, s, 2, :].rearrange("p (k r) -> p k r", k=KT)[:, :, first:end]
                    sp.dma_start(stage[first:end, s, 0, :], gate).then_inc(stage_loaded[s], 16)
                    sp.dma_start(stage[first:end, s, 1, :], up).then_inc(stage_loaded[s], 16)
                    sp.dma_start(dst, down.rearrange("(k p) r -> p k r", p=P)).then_inc(stage_loaded[s], 16)
                if g >= WSLOTS:
                    store_record(g - WSLOTS)
            for g in range(NPREP - WSLOTS, NPREP):
                store_record(g)
            for s in range(WSLOTS):
                sp.wait_ge(rec_stored[s], 16 * len(range(s, NPREP, WSLOTS)))
            sp.sem_inc(route_stored, 16 * RING)
            for s in range(WSLOTS):
                sp.sem_inc(e_stored[s], 16)

            def route_out(layer, c, chunk, routed):
                sp.wait_ge(route_kept, routed + 1)
                sp.sem_inc(past_sp, 1)
                rows = R0 if layer in (F0A, F0B) else R1
                sp.dma_start(route_t.rearrange("r (b s) -> r b s", s=SEQ)[0:rows, chunk, :],
                             wts[c][0:rows, :]).then_inc(route_stored, 16)

            def load_record(layer, t, s, g):
                src = wrec0 if layer in (F0A, F0B) else wrec1
                sp.wait_ge(down_done, 2 * (g - WSLOTS + 1) + RING)
                sp.sem_inc(past_sp, 1)
                sp.dma_start(wslot[:, s, :, :].rearrange("p h w -> p (h w)").bitcast(F32), src[bass.ds(t, 1), :, :].rearrange("t p w -> (t p) w")).then_inc(wrec_in[s], 16)

            def load_routing(pr, r, g, pieces):
                sp.wait_ge(weighted, 2 * (g - RING + 1) + RING)
                sp.sem_inc(past_sp, 1)
                for lo, hi, row in pieces:
                    src = route_t.rearrange("r (q s) -> r q s", s=SEQ)[bass.ds(row, 1), bass.ds(2 * pr, 2), :]
                    sp.dma_start(wbc[lo:hi, r, :, :], src.broadcast_to([hi - lo, 2, SEQ])).then_inc(wbc_in[r], 16)

            def ffn(layer):
                n = TILES[layer]
                with sp.Fori(0, PAIRS_OF) as pr:
                    base = tiles_before(layer, pr)
                    sp.wait_ge(down_done, 2 * base + RING)
                    sp.sem_inc(past_sp, 1)
                    for t in range(WSLOTS):
                        src = wrec0 if layer in (F0A, F0B) else wrec1
                        sp.dma_start(wslot[:, t, :, :].rearrange("p h w -> p (h w)").bitcast(F32), src[t]).then_inc(wrec_in[t], 16)
                    for c in range(2):
                        route_out(layer, c, 2 * pr + c, ROUTED[layer] * NBATCH + 2 * pr + c)
                    sp.wait_ge(route_stored, 16 * (ROUTED[layer] * NBATCH + 2 * pr) + 32 + 16 * RING)
                    sp.sem_inc(past_sp, 1)
                    if layer in (F0A, F0B):
                        for t in range(n):
                            load_routing(pr, t % RING, base + t, split_rows(t, ROWS0, H0, E0))
                            if WSLOTS <= t + LEAD < n:
                                load_record(layer, t + LEAD, (t + LEAD) % WSLOTS, base + t + LEAD)
                    else:
                        rows = [(2 * t, 2 * t + 1) if t < PAIRS else (E1, E1) for t in range(n)]
                        first, turns = WSLOTS - LEAD, PAIRS // WSLOTS - 1
                        for t in range(first):
                            load_routing(pr, t % RING, base + t, [(0, H1, rows[t][0]), (H1, P, rows[t][1])])
                        with sp.Fori(0, turns) as i:
                            for u in range(WSLOTS):
                                t = WSLOTS * i + first + u
                                load_routing(pr, (first + u) % RING, base + t, [(0, H1, 2 * t), (H1, P, 2 * t + 1)])
                                load_record(layer, t + LEAD, u, base + t + LEAD)
                        for t in range(WSLOTS * turns + first, n):
                            load_routing(pr, t % RING, base + t, [(0, H1, rows[t][0]), (H1, P, rows[t][1])])
                            if t + LEAD < n:
                                load_record(layer, t + LEAD, (t + LEAD) % WSLOTS, base + t + LEAD)

            def expert_records():
                gu, dp = a["L1_ffn_gu_w"], a["L1_ffn_dp_w"]
                sp.wait_ge(xn_ready, KT * NBATCH * (ATT + 1))
                with sp.Fori(0, PAIRS // WSLOTS) as h:
                    for u in range(WSLOTS):
                        E = WSLOTS * h + u
                        sp.wait_ge(e_turned, E + 1)
                        sp.sem_inc(past_sp, 1)
                        for q in range(2):
                            e = bass.ds(2 * E + q, 1)
                            rows = slice(q * H1, q * H1 + H1)
                            sp.dma_start(estage[u][rows, 0, :], gu[e, 0:H1, :].rearrange("e i c -> (e i) c")).then_inc(e_loaded[u], 16)
                            sp.dma_start(estage[u][rows, 1, :], gu[e, H1:2 * H1, :].rearrange("e i c -> (e i) c")).then_inc(e_loaded[u], 16)
                            sp.dma_start(estage[u][:, 2, :].rearrange("p (k r) -> p k r", k=KT)[:, :, rows],
                                         dp[e, :, :].rearrange("e (k p) r -> p (e k) r", p=P)).then_inc(e_loaded[u], 16)
                    for u in range(WSLOTS):
                        E = WSLOTS * h + u
                        sp.wait_ge(e_lo, E + 2)
                        sp.sem_inc(past_sp, 1)
                        sp.dma_start(wrec1[bass.ds(E, 1), :, :].rearrange("t p w -> (t p) w"),
                                     wslot[:, u, :, :].rearrange("p h w -> p (h w)").bitcast(F32)).then_inc(e_stored[u], 16)
                for u in range(WSLOTS):
                    sp.wait_ge(e_stored[u], 16 * (PAIRS // WSLOTS) + 16)

            def ssm():
                def move_b(b, j):
                    rows = slice(2 * NST * j, 2 * NST * (j + 1))
                    sp.dma_start(bqh[:, j, :].bitcast(F32), bh_all[rows, b, :].bitcast(F32)).then_inc(bq_in[j], 16)
                    sp.dma_start(bql[:, j, :].bitcast(F32), bl_all[rows, b, :].bitcast(F32)).then_inc(bq_in[j], 16)

                sp.wait_ge(b_lo, 1)
                for j in range(JT):
                    move_b(0, j)
                sp.wait_ge(b_lo, NBATCH)
                with sp.Fori(0, NBATCH - 1) as b:
                    for j in range(JT):
                        sp.wait_ge(bx_done, STEPS * b + NST * (j + 1) + RING)
                        sp.sem_inc(past_sp, 1)
                        move_b(b + 1, j)

            ffn(F0A)
            expert_records()
            ffn(F0B)
            ffn(F1A)
            ssm()
            ffn(F1B)
            orow = out.rearrange("b (t p) c -> p (b t) c", p=P)
            for g in range(8):
                sp.wait_ge(out_kept, g + 1)
                sp.dma_start(orow[:, 2 * g:2 * g + 2, :], outbuf[:, 2 * g:2 * g + 2, :]).then_inc(stored, 16)
            sp.wait_ge(stored, 16 * 8)

        def turned_groups():
            groups = []
            for b in range(NBATCH):
                half = (xnat if b < 2 else xnat2).rearrange("p (t c) -> p t c", c=C)
                for k in range(KT):
                    srcs = [(half[:, (NT * b + i) % 8, k * P:k * P + P], i * P) for i in range(NT)]
                    groups.append((srcs, P, [(xT[:, k, b, :], lambda v: v[:, 0:SEQ])]))
            for r in range(0, 10, 2):
                srcs = [(st_in[:, r + q, k * P:k * P + P], (2 * k + q) * P) for k in range(KT) for q in range(2)]
                whole = lambda v: v[:, 0:SEQ].rearrange("p (k n) -> p k n", k=KT)
                if r < JT:
                    copies = [(w_in[:, :, OZ + r * P:OZ + r * P + 2 * P], whole)]
                elif r == JT:
                    xrep = w_in[:, :, OX:OX + DI].rearrange("p k (h r n) -> p k h r n", h=XH, r=REP)
                    copies = [(xrep[:, k, :, q, :],
                               lambda v, k=k: v[:, 2 * k * P:2 * k * P + P].rearrange("p (h n) -> p h n", h=XH))
                              for k in range(KT) for q in range(REP)]
                    copies.append((w_in[:, :, OB:OB + DXB], lambda v: whole(v)[:, :, P:2 * P]))
                else:
                    copies = [(w_in[:, :, OC + (r - 6) * P:OC + (r - 4) * P], whole)]
                groups.append((srcs, P, copies))
            groups.append(([(st_dtin[:, k * P:k * P + P], k * P) for k in range(KT)], P,
                           [(w_dtin[:, :, :], lambda v: v[:, 0:C].rearrange("p (k n) -> p k n", k=KT))]))
            groups.append(([(st_dt[:, j, :], j * P) for j in range(JT)], P, [(w_dt[:, :], lambda v: v[:, 0:DI])]))
            for h in range(2):
                srcs = [(st_out[:, k, (2 * h + j) * P:(2 * h + j + 1) * P], (2 * j + k) * P)
                        for j in range(2) for k in range(KT)]
                groups.append((srcs, P, [(w_out[:, 2 * h:2 * h + 2, :],
                                          lambda v: v[:, 0:SEQ].rearrange("p (j n) -> p j n", j=2))]))
            for st, gw, n in ((st_g0, gw0, E0), (st_g1, gw1, R1)):
                groups.append(([(st[0:n, k * P:k * P + P], k * n) for k in range(KT)], n,
                               [(gw[:, :, :], lambda v, n=n: v[:, 0:KT * n].rearrange("p (k n) -> p k n", k=KT))]))
            return groups

        TURNED = turned_groups()
        NX = NBATCH * KT

        def turned_after(g):
            per = -(-len(TURNED) // NPREP)
            return list(enumerate(TURNED))[per * g:per * g + per]

        UNITS = []
        for h in range(0, HEADS, 2):
            UNITS += [[(3, h, 0, 4)], [(2, h, 0, 3), (0, h, 3, 1)],
                      [(3, h + 1, 0, 4)], [(2, h + 1, 0, 3), (0, h + 1, 3, 1)],
                      [(1, h, 0, 2), (1, h + 1, 2, 2)]]
        NU = len(UNITS)
        PER_PAIR = NU // EPB

        @block.gpsimd
        def _(pool):
            done = [0]

            def link(ins):
                done[0] += 1
                ins.then_inc(consts, 1)
                pool.wait_ge(consts, done[0])

            selt = arena[:, 8192:8192 + NST * P]
            selt_b = arena[:, 8192 + NST * P:8192 + 2 * NST * P]
            link(pool.memset(ident[:], 0.0))
            link(pool.affine_select(out=ident[:], in_=ident[:], compare_op=ALU.not_equal, fill=1.0, base=0,
                                    pattern=[[-1, P]], channel_multiplier=1))
            link(pool.memset(ones[:], 1.0 / C))
            link(pool.memset(epsc[:], EPS))
            link(pool.memset(maskb[:], 0.0))
            link(pool.affine_select(out=maskb[:], in_=maskb[:], compare_op=ALU.is_ge, fill=NEG, base=0,
                                    pattern=[[-1, P]], channel_multiplier=1))
            link(pool.tensor_copy(identb[:], ident[:]))
            link(pool.memset(headmask[:], 1.0))
            link(pool.affine_select(out=headmask[:], in_=headmask[:], compare_op=ALU.is_ge, fill=0.0, base=0,
                                    pattern=[[-HD, HPT]], channel_multiplier=1))
            link(pool.affine_select(out=headmask[:], in_=headmask[:], compare_op=ALU.is_ge, fill=0.0, base=HD - 1,
                                    pattern=[[HD, HPT]], channel_multiplier=-1))
            for e in range(E0):
                link(pool.memset(iota0[:, e:e + 1], float(e)))
            link(pool.memset(selt, 0.0))
            link(pool.affine_select(out=selt.rearrange("p (n h m) -> p n h m", n=NST, h=HPT),
                                    in_=selt.rearrange("p (n h m) -> p n h m", n=NST, h=HPT),
                                    compare_op=ALU.not_equal, fill=1.0, base=0,
                                    pattern=[[1, NST], [NST, HPT], [0, NST]], channel_multiplier=-1))
            link(pool.tensor_copy(sel_c[:, :, :].rearrange("p n m -> p (n m)"), selt))
            link(pool.memset(selt_b, 0.0))
            link(pool.affine_select(out=selt_b.rearrange("p (n h m) -> p n h m", n=NST, h=2),
                                    in_=selt_b.rearrange("p (n h m) -> p n h m", n=NST, h=2),
                                    compare_op=ALU.not_equal, fill=1.0, base=0,
                                    pattern=[[1, NST], [NST, 2], [0, 64]], channel_multiplier=-1))
            link(pool.tensor_copy(sel_b[:, :, :].rearrange("p n m -> p (n m)"), selt_b[0:2 * NST, :]))
            assert done[0] == NCONST
            for g in (TILES0 - 1, NPREP - 1):
                s, r = g % WSLOTS, padding(g)
                pool.wait_ge(rec_turned, g - WSLOTS + 1)
                if g >= TILES0:
                    pool.wait_ge(padded, 2)
                pool.memset(stage[r:P, s, 0:2, :], 0.0).then_inc(padded, 1)
                pool.wait_ge(padded, 1 if g < TILES0 else 3)
                pool.memset(stage[:, s, 2, :].rearrange("p (k r) -> p k r", k=KT)[:, :, r:P], 0.0).then_inc(padded, 1)
            pool.sem_inc(weighted, RING)
            pool.sem_inc(y_added, RING)
            pool.sem_inc(y_gated, 1)

            def weigh(q, c, r):
                pool.wait_ge(prod_done, q + 1 + RING)
                pool.wait_ge(hid_lo, q + 1)
                pool.tensor_tensor(iw[:, c, :], prod[:, c, :], wbc[:, r, c, :], ALU.mult).then_inc(weighted, 1)

            def tile(layer, pr, t, r, nth, base):
                pool.wait_ge(wbc_in[r], 32 * (ring_count(layer, pr, r) + nth + 1))
                for c in range(2):
                    weigh(2 * (base + t) + c, c, r)

            def ffn(layer):
                n = TILES[layer]
                with pool.Fori(0, PAIRS_OF) as pr:
                    base = tiles_before(layer, pr)
                    with pool.Fori(0, n // RING) as i:
                        for u in range(RING):
                            tile(layer, pr, RING * i + u, u, i, base)
                    for t in range(n // RING * RING, n):
                        tile(layer, pr, t, t % RING, t // RING, base)

            def ssm():
                def times_x(N, r):
                    pool.wait_ge(proj_taken, JOBS * N + 3 + RING)
                    pool.wait_ge(dt_done, N + 1)
                    pool.tensor_tensor(dtx[:, r, :], dt[:, r, :], xact[:, r, :], ALU.mult).then_inc(dtx_done, 1)

                times_x(0, 0)
                with pool.Fori(0, NBATCH) as b:
                    for j in range(JT):
                        J, r = JT * b + j, j % RING
                        pool.wait_ge(skip_set, J + 1)
                        for n in range(NST):
                            s = STEPS * b + NST * j + n
                            pool.wait_ge(hc_done, s + 1 + RING)
                            pool.wait_ge(y_added, s + RING)
                            pool.tensor_tensor(xact[:, r, :], xact[:, r, :], hc[:, n % RING, :], ALU.add).then_inc(y_added, 1)
                            if n == POOL_AT["dtx"]:
                                times_x(J + 1, (j + 1) % RING)
                        pool.wait_ge(y_added, NST * J + NST + RING)
                        pool.tensor_tensor(xact[:, r, :], xact[:, r, :], zg[:, r, :], ALU.mult).then_inc(y_gated, 1)

            def attention():
                pool.wait_ge(xn_ready, KT * NBATCH * (ATT + 1))
                pool.tensor_copy(xn[:, 0, :, :], xns[:, 0, :, :]).then_inc(xn_copied, 1)
                with pool.Fori(0, NBATCH - 1) as b:
                    pool.wait_ge(qkv_ready, 4 * b + 4)
                    pool.sem_inc(past_pool, 1)
                    pool.tensor_copy(xn[:, 0, :, :], xns[:, b + 1, :, :]).then_inc(xn_copied, 1)

            ffn(F0A)
            attention()
            ffn(F0B)
            ffn(F1A)
            ssm()
            ffn(F1B)

        @block.tensor
        def _(pe):
            pe.wait_ge(consts, 2)
            for g in range(NPREP):
                s, bank = g % WSLOTS, 2 * (g % RING)
                pe.wait_ge(stage_loaded[s], stage_count(g))
                if padding(g) < P:
                    pe.wait_ge(padded, 2 if g < TILES0 else 4)
                pe.wait_ge(rec_lo, g + 1)
                for w in range(2):
                    for k in range(KT):
                        pe.transpose(ps[:, bank, (2 * k + w) * P:(2 * k + w + 1) * P], stage[:, s, w, k * P:k * P + P], ident[:])
                for k in range(KT):
                    last = pe.transpose(ps[:, bank + 1, k * P:k * P + P], stage[:, s, 2, k * P:k * P + P], ident[:])
                last.then_inc(rec_turned, 1)
                for n, (srcs, rows, _) in turned_after(g):
                    if n == 0:
                        pe.wait_ge(x_loaded, 32)
                    if n == NX:
                        pe.wait_ge(w_loaded, 16 * 7)
                    if n >= RING:
                        pe.wait_ge(m_kept, n - RING + 1)
                    for src, at in srcs:
                        last = pe.transpose(ps[:, 4 + n % RING, at:at + rows], src, ident[0:rows, 0:rows])
                    last.then_inc(m_turned, 1)
            pe.sem_inc(down_done, RING)
            pe.sem_inc(e_turned, WSLOTS)
            pe.sem_inc(c_spread, RING)
            pe.sem_inc(route_turned, 1)
            pe.sem_inc(prob_turned, RING)
            pe.sem_inc(pv_done, RING)

            def product(bank, pairs, start=True, stop=True):
                for n, (w, v) in enumerate(pairs):
                    last = pe.matmul(bank, w, v, start=start and n == 0, stop=stop and n == len(pairs) - 1)
                return last

            def normalise(layer, b, c, x_count):
                R = layer * NBATCH + b
                pe.wait_ge(x_updated, x_count + 1)
                product(ps[:, 4 + c, :], [(ones[:], xT[:, k, b, :]) for k in range(KT)]).then_inc(mean_ready, 1)
                return R

            def variance(R, c):
                pe.wait_ge(squared, R + 1)
                product(ps[:, 6 + c, :], [(ones[:], sq[:, c, k, :]) for k in range(KT)]).then_inc(var_ready, 1)

            def normalise_all(layer):
                for b in range(0, NBATCH, 2):
                    if b:
                        pe.wait_ge(centred, KT * (layer * NBATCH + b))
                    Rs = [normalise(layer, b + c, c, x_before(layer)) for c in range(2)]
                    if b:
                        pe.wait_ge(log_done, layer * NBATCH + b)
                    for c in range(2):
                        variance(Rs[c], c)

            def route(layer, R, c, routed):
                gw, E = (gw0, E0) if layer in (F0A, F0B) else (gw1, R1)
                pe.wait_ge(xn_ready, KT * (R + 1))
                for i in range(NT):
                    last = product(ps[:, 2 + c, i * E:i * E + E],
                                   [(xn[:, c, k, i * P:i * P + P], gw[:, k, :]) for k in range(KT)])
                last.then_inc(logits_ready, 1)

            def route_turn(layer, c, routed):
                rows = R0 if layer in (F0A, F0B) else R1
                pe.wait_ge(route_ready, routed + 2)
                for i in range(NT):
                    last = pe.transpose(ps[0:rows, c, i * P:i * P + P], wr[:, i, 0:rows], ident[:])
                last.then_inc(route_turned, 1)

            def gate_up(q, c, s):
                pe.wait_ge(silu_done, q + 1)
                for w, bank, free, ready in ((0, 4 + c, silu_done, gate_ready), (1, 6 + c, prod_done, up_ready)):
                    if w:
                        pe.wait_ge(prod_done, q + 1)
                    pairs = []
                    for k in range(KT):
                        at = slice((2 * k + w) * P, (2 * k + w + 1) * P)
                        pairs += [(wslot[:, s, 0, at], xnh[:, c, k, :]), (wslot[:, s, 0, at], xnl[:, c, k, :]),
                                  (wslot[:, s, 1, at], xnh[:, c, k, :])]
                    product(ps[:, bank, :], pairs).then_inc(ready, 1)

            def down(q, c, s, start=False, stop=False):
                pe.wait_ge(hid_lo, q + 1 + RING)
                for k in range(KT):
                    at = slice(2 * KT * P + k * P, 2 * KT * P + k * P + P)
                    for n, (w, v) in enumerate(((wslot[:, s, 0, at], iwh[:, c, :]), (wslot[:, s, 0, at], iwl[:, c, :]),
                                                (wslot[:, s, 1, at], iwh[:, c, :]))):
                        last = pe.matmul(ps[:, 2 * c + k, :], w, v, start=start and n == 0, stop=stop and n == 2,
                                         skip_group_check=True)
                last.then_inc(down_done, 1)

            def ffn(layer):
                n = TILES[layer]
                Rs = [normalise(layer, c, c, x_before(layer)) for c in range(2)]
                for pr in range(PAIRS_OF):
                    base = tiles_before(layer, pr)
                    for c in range(2):
                        variance(Rs[c], c)
                    pe.wait_ge(x_updated, x_before(layer) + 2 * KT * pr + 1)
                    for c in range(2):
                        route(layer, Rs[c], c, None)
                    pe.wait_ge(xn_lo, ROUTED[layer] * NBATCH + 2 * pr + 2)

                    def both(t, s, sprev, nth):
                        pe.wait_ge(wrec_in[s], 16 * (slot_count(layer, pr, s) + nth + 1))
                        for c in range(2):
                            down(2 * (base + t) - 2 + c, c, sprev)
                            gate_up(2 * (base + t) + c, c, s)

                    pe.wait_ge(wrec_in[0], 16 * (slot_count(layer, pr, 0) + 1))
                    for c in range(2):
                        gate_up(2 * base + c, c, 0)
                        route_turn(layer, c, ROUTED[layer] * NBATCH + 2 * pr + c)
                    pe.wait_ge(wrec_in[1], 16 * (slot_count(layer, pr, 1) + 1))
                    for c in range(2):
                        gate_up(2 * (base + 1) + c, c, 1)
                    pe.wait_ge(route_kept, ROUTED[layer] * NBATCH + 2 * pr + 2)
                    for c in range(2):
                        down(2 * base + c, c, 0, start=True)
                    turns = (n - 2) // WSLOTS
                    with pe.Fori(0, turns) as i:
                        for u in range(WSLOTS):
                            s = (u + 2) % WSLOTS
                            both(WSLOTS * i + u + 2, s, (u + 1) % WSLOTS, i + (u + 2) // WSLOTS)
                    for t in range(turns * WSLOTS + 2, n):
                        both(t, t % WSLOTS, (t - 1) % WSLOTS, t // WSLOTS)
                    if pr < PAIRS_OF - 1:
                        pe.wait_ge(silu_done, 2 * (base + n) + RING)
                        Rs = [normalise(layer, 2 * pr + 2 + c, c, x_before(layer)) for c in range(2)]
                    for c in range(2):
                        down(2 * (base + n) - 2 + c, c, (n - 1) % WSLOTS, stop=True)

            def attention():
                normalise_all(ATT)
                pe.wait_ge(centred, KT * NBATCH * (ATT + 1))
                pe.wait_ge(log_done, NBATCH * (ATT + 1))
                with pe.Fori(0, NBATCH) as b:
                    pe.wait_ge(xn_copied, b + 1)
                    product(ps[:, 2, :], [(wk[:, k, :, :].rearrange("p m d -> p (m d)"), xn[:, 0, k, :]) for k in range(KT)]).then_inc(qkv_ready, 1)
                    pe.wait_ge(e_lo, EPB * b + 1)
                    for m in range(KT):
                        product(ps[:, m, :], [(wq[:, k, m * P:m * P + P], xn[:, 0, k, :]) for k in range(KT)]).then_inc(qkv_ready, 1)
                    for i in range(NT):
                        last = product(ps[:, 3, i * HD:i * HD + HD],
                                       [(xn[:, 0, k, i * P:i * P + P], wv[:, k, :]) for k in range(KT)])
                    last.then_inc(qkv_ready, 1)
                    pe.wait_ge(q_kept, KT * (b + 1))
                    pe.wait_ge(k_kept, HPT * (b + 1))
                    pe.wait_ge(v_kept, b + 1)

                    def scores(u):
                        U = NU * b + u
                        pe.wait_ge(prob_ready, U + 1)
                        for i, h, at, n in UNITS[u]:
                            pe.matmul(ps[:, 4 + u % RING, at * P:(at + n) * P], qT[:, h // HPT, i * P:i * P + P],
                                      kpad[:, h % HPT, 0:n * P], start=True, stop=False)
                            last = pe.matmul(ps[:, 4 + u % RING, (at + n - 1) * P:(at + n) * P], identb[:], maskb[:],
                                             start=False, stop=True)
                        last.then_inc(score_ready, 1)

                    def turn(u):
                        U = NU * b + u
                        pe.wait_ge(prob_ready, U + 1 + RING)
                        pe.wait_ge(probT_kept, U + 1)
                        for m in range(NT):
                            last = pe.transpose(ps[:, 6 + u % RING, m * P:m * P + P], prob[:, u % RING, m * P:m * P + P], ident[:])
                        last.then_inc(prob_turned, 1)

                    def values(u):
                        U = NU * b + u
                        pe.wait_ge(probT_kept, U + 1 + RING)
                        for i, h, at, n in UNITS[u]:
                            col = (i % 2) * C + h * HD
                            last = product(ps[:, 2 + i // 2, col:col + HD],
                                           [(probT[:, u % RING, (at + m) * P:(at + m + 1) * P], vt[:, m, :]) for m in range(n)])
                        last.then_inc(pv_done, 1)

                    def turn_experts(i):
                        s = i % WSLOTS
                        pe.wait_ge(e_loaded[s], 96 * (EPB // WSLOTS * b + i // WSLOTS) + 96)
                        pe.wait_ge(e_lo, EPB * b + i + 1)
                        for w in range(2):
                            for k in range(KT):
                                pe.transpose(ps[:, 0, (2 * k + w) * P:(2 * k + w + 1) * P], estage[s][:, w, k * P:k * P + P], ident[:])
                        for k in range(KT):
                            last = pe.transpose(ps[:, 1, k * P:k * P + P], estage[s][:, 2, k * P:k * P + P], ident[:])
                        last.then_inc(e_turned, 1)

                    for u in range(NU + 3):
                        if u < NU:
                            scores(u)
                        if u < NU and u % PER_PAIR == 1:
                            turn_experts(u // PER_PAIR)
                        if 2 <= u < NU + 2:
                            turn(u - 2)
                        if u >= 3:
                            values(u - 3)
                    pe.wait_ge(o_normed, 2 * (b + 1))
                    for m in range(KT):
                        for i in range(NT):
                            last = pe.transpose(ps[:, 4 + m, i * P:i * P + P], osb[:, i, m * P:m * P + P], ident[:])
                        last.then_inc(o_turned, 1)
                    pe.wait_ge(o_kept, KT * (b + 1))
                    for k in range(KT):
                        last = product(ps[:, 6 + k, :], [(wo[:, m, k * P:k * P + P], oT[:, m, :]) for m in range(KT)])
                    last.then_inc(attn_out, 1)

            def ssm():
                normalise_all(SSM)
                for b in range(NBATCH):
                    if b >= 2:
                        pe.wait_ge(b_lo, b - 1)
                        pe.wait_ge(dt_in_kept, b - 1)
                    pe.wait_ge(xn_ready, KT * (SSM * NBATCH + b + 1))
                    product(ps[:, (2 * b) % 4, :], [(w_in[:, k, OB:OB + P], xns[:, b, k, :]) for k in range(KT)]).then_inc(b_ready, 1)
                    product(ps[:, (2 * b + 1) % 4, :], [(w_dtin[:, k, :], xns[:, b, k, :]) for k in range(KT)]).then_inc(dt_in_ready, 1)

                def project(N, m, b, j, part):
                    if part == 0:
                        pe.wait_ge(proj_taken, JOBS * N + max(m, 1) + 1)
                        if m == 0:
                            pe.wait_ge(dt_in_kept, NBATCH)
                        if m == 2:
                            pe.wait_ge(proj_taken, JOBS * N + 2 + RING)
                        pe.sem_inc(past_pe, 1)
                    if m == 0:
                        w, v = w_dt[:, j * P:(j + 1) * P], dt_in[:, b, :]
                    elif m == 2:
                        w, v = convd[:, TAPS * j + part, :], xpad[:, j % RING, part:part + SEQ]
                    else:
                        at = {1: OX, 3: OC, 4: OZ}[m] + j * P
                        w, v = w_in[:, part, at:at + P], xns[:, b, part, :]
                    last = pe.matmul(ps[:, PROJ_BANK[m], :], w, v, start=part == 0, stop=part == PARTS[m] - 1,
                                     skip_group_check=True)
                    if part == PARTS[m] - 1:
                        last.then_inc(proj_ready, 1)

                def put_out(J, j, k):
                    if k == 0:
                        pe.wait_ge(y_gated, J + 1)
                        pe.wait_ge(x_updated, x_before(SSM) + KT * J + 1)
                    pe.matmul(ps[:, 6 + k, :], w_out[:, (j - 1) % JT, k * P:k * P + P], xact[:, (j - 1) % RING, :]).then_inc(y_out, 1)

                pe.wait_ge(diagonals, JT * TAPS)
                pe.wait_ge(centred, KT * NBATCH * (SSM + 1))
                pe.wait_ge(log_done, NBATCH * (SSM + 1))
                for m in range(JOBS):
                    for part in range(PARTS[m]):
                        project(0, m, 0, 0, part)
                pe.wait_ge(b_lo, NBATCH)
                with pe.Fori(0, NBATCH) as b:
                    after = (b + 1) % NBATCH
                    for j in range(JT):
                        J = JT * b + j
                        ahead = (J + 1, b, j + 1) if j < JT - 1 else (J + 1, after, 0)

                        pe.wait_ge(bq_in[j], 32 * b + 32)
                        pe.wait_ge(c_lo, J + 1)
                        for n in range(NST):
                            s = STEPS * b + NST * j + n
                            pe.wait_ge(bx_done, s + 1)
                            product(ps[:, n % RING, :], [(sel_b[:, n, :], bqh[:, j, :]), (sel_b[:, n, :], bql[:, j, :])]).then_inc(b_spread, 1)
                            pe.wait_ge(hc_done, s + 1)
                            product(ps[:, 2 + n % RING, :], [(sel_c[:, n, :], iwh[:, j % RING, :]), (sel_c[:, n, :], iwl[:, j % RING, :])]).then_inc(c_spread, 1)
                            for m, name in enumerate(JOB_NAMES):
                                if 0 <= n - PE_AT[name] < PARTS[m]:
                                    project(ahead[0], m, ahead[1], ahead[2], n - PE_AT[name])
                            if 0 <= n - PE_AT["put"] < KT:
                                put_out(J, j, n - PE_AT["put"])
                for k in range(KT):
                    put_out(NBATCH * JT, 0, k)
                pe.wait_ge(proj_taken, JOBS * (NBATCH * JT + 1) + RING)

            pe.wait_ge(consts, NCONST)
            pe.wait_ge(small_ready, 3)
            pe.wait_ge(m_kept, len(TURNED))
            pe.wait_ge(rec_lo, NPREP + RING)
            pe.wait_ge(small_loaded, 160)
            ffn(F0A)
            attention()
            ffn(F0B)
            ffn(F1A)
            ssm()
            ffn(F1B)
            pe.wait_ge(x_updated, x_before(6) + 1)
            for g in range(8):
                if g >= RING:
                    pe.wait_ge(out_kept, g - RING + 1)
                for i in range(2):
                    t = 2 * g + i
                    for k in range(KT):
                        last = pe.transpose(ps[:, g % RING, i * C + k * P:i * C + k * P + P],
                                            xT[:, k, t // NT, (t % NT) * P:(t % NT + 1) * P], ident[:])
                last.then_inc(out_turned, 1)

        @block.scalar
        def _(act):
            with nc.allow_non_contiguous_dma(reason="columns of 512 parameters, once"):
                act.dma_start(bias0[:], a["L0_ffn_gate_bias"].rearrange("(o e) -> o e", o=1).broadcast_to([P, E0])).then_inc(small_loaded, 16)
                act.dma_start(conv_w[:], a["L1_attn_conv_w"].rearrange("(j p) k -> p j k", p=P)).then_inc(small_loaded, 16)
                act.dma_start(conv_b[:], a["L1_attn_conv_b"].rearrange("(j p) -> p j", p=P)).then_inc(small_loaded, 16)
                act.dma_start(dt_b[:], a["L1_attn_dt_proj_b"].rearrange("(j p) -> p j", p=P)).then_inc(small_loaded, 16)
                act.dma_start(d_skip[:], a["L1_attn_D"].rearrange("(j p) -> p j", p=P)).then_inc(small_loaded, 16)
                act.dma_start(a_neg[:], a["L1_attn_A_log"].rearrange("(j p) n -> p j n", p=P)).then_inc(small_loaded, 16)
                act.dma_start(wq[:], a["L0_attn_Wq"].rearrange("(k p) n -> p k n", p=P)).then_inc(small_loaded, 16)
                act.dma_start(wo[:], a["L0_attn_Wo"].rearrange("(k p) n -> p k n", p=P)).then_inc(small_loaded, 16)
                act.dma_start(wk[:, :, 0, :], a["L0_attn_Wk"].rearrange("(k p) n -> p k n", p=P)).then_inc(small_loaded, 16)
                act.dma_start(wv[:], a["L0_attn_Wv"].rearrange("(k p) n -> p k n", p=P)).then_inc(small_loaded, 16)
            act.wait_ge(small_loaded, 160)
            act.activation(a_neg[:], a_neg[:], ACT.Exp).then_inc(a_ready, 1)
            for g in range(NPREP):
                s, bank = g % WSLOTS, 2 * (g % RING)
                act.wait_ge(rec_turned, g + 1)
                if g >= WSLOTS:
                    act.wait_ge(rec_stored[s], 16 * (g // WSLOTS))
                act.activation(wslot[:, s, 0, :], ps[:, bank:bank + 2, :].rearrange("p k s -> p (k s)")[:, 0:REC],
                               ACT.Copy).then_inc(rec_hi, 1)
            act.sem_inc(silu_done, RING)
            act.sem_inc(proj_taken, RING)
            act.sem_inc(prob_ready, RING)

            def spread(layer, b, cs, into=None):
                R = [layer * NBATCH + b + c for c in cs]
                for c in cs:
                    act.wait_ge(centred, KT * (R[c] + 1))
                    act.activation(sq[:, c, :, :], xn[:, c, :, :] if into is None else into[c], ACT.Square).then_inc(squared, 1)
                for c in cs:
                    act.wait_ge(var_ready, R[c] + 1)
                    act.activation(sq[:, c, 0, :], ps[:, 6 + c, :], ACT.Ln, bias=epsc[:, 0:1]).then_inc(log_done, 1)
                for c in cs:
                    act.wait_ge(log_done, R[c] + 1)
                    act.activation(sq[:, c, 0, :], sq[:, c, 0, :], ACT.Exp, scale=-0.5).then_inc(rstd_ready, 1)
                return R

            def spread_all(layer):
                for b in range(0, NBATCH, 2):
                    if b:
                        act.wait_ge(xn_ready, KT * (layer * NBATCH + b))
                    spread(layer, b, (0, 1), [xns[:, b + c, :, :] for c in range(2)])

            def silu(q, c):
                act.wait_ge(gate_ready, q + 1)
                act.wait_ge(prod_done, q + 1)
                act.activation(gact[:, c, :], ps[:, 4 + c, :], ACT.Silu).then_inc(silu_done, 1)

            def hidden_hi(q, c):
                act.wait_ge(weighted, q + 1 + RING)
                act.wait_ge(down_done, q + 1)
                act.activation(iwh[:, c, :], iw[:, c, :], ACT.Copy).then_inc(hid_hi, 1)

            def ffn(layer):
                n = TILES[layer]
                with act.Fori(0, PAIRS_OF) as pr:
                    base = tiles_before(layer, pr)
                    R = spread(layer, 2 * pr, (0, 1))
                    for c in range(2):
                        act.wait_ge(xn_ready, KT * (R[c] + 1))
                        act.activation(xnh[:, c, :, :], xn[:, c, :, :], ACT.Copy).then_inc(xn_hi, 1)
                    for c in range(2):
                        routed = ROUTED[layer] * NBATCH + 2 * pr + c
                        if layer in (F0A, F0B):
                            act.wait_ge(logits_ready, routed + 1)
                            act.wait_ge(route_ready, routed + 1)
                            act.activation(ex[:, :, 0:E0], ps[:, 2 + c, 0:NT * E0].rearrange("p (i e) -> p i e", i=NT),
                                           ACT.Exp, scale=-1.0).then_inc(route_exp, 1)
                        else:
                            act.wait_ge(route_dve, dve_route_before(layer, 2 * pr + c) + 11)
                            act.activation(ex[:, :, 0:E1], ex[:, :, 0:E1], ACT.Exp)
                            act.activation(ex[:, :, E1:R1], lg[:, :, E1:R1], ACT.Exp, scale=-1.0).then_inc(route_exp, 1)
                    for c in range(2):
                        routed = ROUTED[layer] * NBATCH + 2 * pr + c
                        rows = R0 if layer in (F0A, F0B) else R1
                        act.wait_ge(route_turned, routed + 2)
                        act.wait_ge(route_stored, 16 * routed + 16)
                        act.activation(wts[c][0:rows, :], ps[0:rows, c, :], ACT.Copy).then_inc(route_kept, 1)
                    act.activation(tiny[:, 0:1], epsc[:, 0:1], ACT.Silu)
                    with act.Fori(0, n) as t:
                        for c in range(2):
                            silu(2 * (base + t) + c, c)
                            hidden_hi(2 * (base + t) + c, c)

            def attention():
                spread_all(ATT)
                with act.Fori(0, NBATCH) as b:
                    for m in range(KT):
                        act.wait_ge(qkv_ready, 4 * b + m + 2)
                        act.activation(qT[:, m, :], ps[:, m, :], ACT.Copy).then_inc(q_kept, 1)
                    act.wait_ge(qkv_ready, 4 * (b + 1))
                    act.activation(vt[:, :, :], ps[:, 3, 0:NT * HD].rearrange("p (i d) -> p i d", i=NT), ACT.Copy).then_inc(v_kept, 1)
                    act.wait_ge(inv_ready, b + 1)
                    for u in range(NU):
                        U, r = NU * b + u, u % RING
                        act.wait_ge(negmax, U + 1)
                        act.wait_ge(prob_turned, U + 1)
                        for p, (i, h, at, n) in enumerate(UNITS[u]):
                            last = act.activation(prob[:, r, at * P:(at + n) * P], ps[:, 4 + r, at * P:(at + n) * P], ACT.Exp,
                                                  bias=nb[:, r, p:p + 1], scale=SCALE, accum_out=psums[:, i, h:h + 1])
                        last.then_inc(prob_ready, 1)
                        if u % PER_PAIR == 2:
                            i = u // PER_PAIR
                            act.wait_ge(e_turned, EPB * b + i + 1 + WSLOTS)
                            act.wait_ge(e_stored[i % WSLOTS], 16 * (EPB // WSLOTS * b + i // WSLOTS) + 16)
                            act.activation(wslot[:, i % WSLOTS, 0, :], ps[:, 0:2, :].rearrange("p k s -> p (k s)")[:, 0:REC],
                                           ACT.Copy).then_inc(e_hi, 1)
                    for m in range(KT):
                        act.wait_ge(o_turned, KT * b + m + 1)
                        act.activation(oT[:, m, :], ps[:, 4 + m, :], ACT.Copy).then_inc(o_kept, 1)

            def ssm():
                spread_all(SSM)
                for b in range(NBATCH):
                    act.wait_ge(b_ready, b + 1)
                    act.activation(bh_all[:, b, :], ps[:, (2 * b) % 4, :], ACT.Copy).then_inc(b_hi, 1)
                    act.wait_ge(dt_in_ready, b + 1)
                    act.activation(dt_in[:, b, :], ps[:, (2 * b + 1) % 4, :], ACT.Copy).then_inc(dt_in_kept, 1)

                def take(N, m, r, j, ring):
                    act.wait_ge(proj_ready, JOBS * N + m + 1)
                    bank = ps[:, PROJ_BANK[m], :]
                    if m == 0:
                        act.activation(dt[:, r, :], bank, ACT.Identity, bias=dt_b[:, j:j + 1]).then_inc(proj_taken, 1)
                    elif m == 1:
                        if ring:
                            act.wait_ge(bx_done, NST * (N - 1) + RING)
                        act.activation(xpad[:, r, TAPS - 1:XPAD], bank, ACT.Copy).then_inc(proj_taken, 1)
                    elif m == 2:
                        if ring:
                            act.wait_ge(y_out, KT * N)
                        act.activation(xact[:, r, :], bank, ACT.Silu, bias=conv_b[:, j:j + 1]).then_inc(proj_taken, 1)
                    elif m == 3:
                        if ring:
                            act.wait_ge(c_spread, NST * (N - 1) + RING)
                        act.activation(iwh[:, r, :], bank, ACT.Copy).then_inc(proj_taken, 1)
                    else:
                        if ring:
                            act.wait_ge(y_gated, N)
                        act.activation(zg[:, r, :], bank, ACT.Silu).then_inc(proj_taken, 1)

                def exp_abs(N, r, ring):
                    act.wait_ge(proj_taken, JOBS * N + 1 + RING)
                    if ring:
                        act.wait_ge(dt_done, N)
                    act.activation(sp_e, dt[:, r, :], ACT.Abs).then_inc(dt_abs, 1)
                    act.wait_ge(dt_abs, N + 1)
                    act.activation(sp_e, sp_e, ACT.Exp, scale=-1.0).then_inc(dt_exp, 1)

                def log_one(N):
                    act.wait_ge(dt_one, N + 1)
                    act.activation(sp_l, sp_1, ACT.Ln).then_inc(dt_log, 1)

                for m in range(JOBS):
                    take(0, m, 0, 0, False)
                exp_abs(0, 0, False)
                log_one(0)
                act.activation(tiny[:, 1:2], epsc[:, 0:1], ACT.Exp)
                with act.Fori(0, NBATCH) as b:
                    for j in range(JT):
                        J, r = JT * b + j, j % RING
                        N, rn, jn = J + 1, (j + 1) % RING, (j + 1) % JT
                        act.wait_ge(dt_done, J + 1)
                        for n in range(NST):
                            s = STEPS * b + NST * j + n
                            act.wait_ge(scanned, s + 1)
                            act.activation(da[:, n % DECAYS, :], dt[:, r, :], ACT.Exp, scale=a_neg[:, j, n:n + 1]).then_inc(decay_ready, 1)
                            if n == ACT_AT["skip"]:
                                act.wait_ge(dtx_done, J + 1)
                                act.activation(xact[:, r, :], xact[:, r, :], ACT.Copy, scale=d_skip[:, j:j + 1]).then_inc(skip_set, 1)
                            if n == ACT_AT["dt"]:
                                take(N, 0, rn, jn, True)
                                exp_abs(N, rn, True)
                            if n == ACT_AT["x"]:
                                take(N, 1, rn, jn, True)
                            if n == ACT_AT["log"]:
                                log_one(N)
                            if n == ACT_AT["conv"]:
                                take(N, 2, rn, jn, True)
                            if n == ACT_AT["C"]:
                                take(N, 3, rn, jn, True)
                            if n == ACT_AT["z"]:
                                take(N, 4, rn, jn, True)

            ffn(F0A)
            attention()
            ffn(F0B)
            ffn(F1A)
            ssm()
            ffn(F1B)

        @block.vector
        def _(dve):
            dve.sem_inc(rec_lo, RING)
            dve.sem_inc(e_lo, 1)
            dve.sem_inc(x_updated, 1)
            dve.sem_inc(prod_done, RING)
            dve.sem_inc(hid_lo, RING)
            dve.sem_inc(probT_kept, RING)
            dve.sem_inc(inv_ready, 1)
            dve.sem_inc(route_ready, 1)
            dve.sem_inc(bx_done, RING)
            dve.sem_inc(hc_done, RING)
            dve.sem_inc(scanned, DECAYS)
            dve.wait_ge(small_loaded, 160)
            for k in range(KT):
                dve.tensor_copy(wk[:, k, 1:HPT, :], wk[:, k, 0:1, :].broadcast_to([P, HPT - 1, HD])).then_inc(small_ready, 1)
            dve.wait_ge(a_ready, 1)
            dve.tensor_scalar(a_neg[:], a_neg[:], -1.0, None, ALU.mult).then_inc(small_ready, 1)
            for g in range(NPREP):
                s, bank = g % WSLOTS, 2 * (g % RING)
                dve.wait_ge(rec_hi, g + 1)
                dve.tensor_tensor(wslot[:, s, 1, :], ps[:, bank:bank + 2, :].rearrange("p k s -> p (k s)")[:, 0:REC],
                                  wslot[:, s, 0, :], ALU.subtract).then_inc(rec_lo, 1)
                for n, (_, rows, copies) in turned_after(g):
                    dve.wait_ge(m_turned, n + 1)
                    for dst, view in copies:
                        last = dve.tensor_copy(dst, view(ps[:, 4 + n % RING, :]))
                    last.then_inc(m_kept, 1)

            def centre(layer, b, cs, into=None):
                for c in cs:
                    dve.wait_ge(mean_ready, layer * NBATCH + b + c + 1)
                    for k in range(KT):
                        v = xn[:, c, k, :] if into is None else into[c][:, k, :]
                        dve.tensor_tensor(v, xT[:, k, b + c, :], ps[:, 4 + c, :], ALU.subtract).then_inc(centred, 1)

            def scale(layer, b, cs, into=None):
                for c in cs:
                    dve.wait_ge(rstd_ready, layer * NBATCH + b + c + 1)
                    for k in range(KT):
                        v = xn[:, c, k, :] if into is None else into[c][:, k, :]
                        dve.tensor_tensor(v, v, sq[:, c, 0, :], ALU.mult).then_inc(xn_ready, 1)

            def normalise_all(layer):
                for b in range(0, NBATCH, 2):
                    into = [xns[:, b + c, :, :] for c in range(2)]
                    centre(layer, b, (0, 1), into)
                    scale(layer, b, (0, 1), into)

            def route(layer, chunk, c):
                routed = ROUTED[layer] * NBATCH + chunk
                start = dve_route_before(layer, chunk)
                done = [0]

                def link(ins):
                    done[0] += 1
                    ins.then_inc(route_dve, 1)
                    return ins

                def after():
                    dve.wait_ge(route_dve, start + done[0])

                dve.wait_ge(logits_ready, routed + 1)
                if layer in (F0A, F0B):
                    E = E0
                    dve.wait_ge(route_exp, ROUTED_EXP(layer, chunk) + 1)
                    link(dve.tensor_scalar(ex[:, :, 0:E], ex[:, :, 0:E], 1.0, None, ALU.add))
                    after()
                    link(dve.reciprocal(lg[:, :, 0:E], ex[:, :, 0:E]))
                    after()
                    link(dve.tensor_tensor(mk[:, :, 0:E], lg[:, :, 0:E], bias0[:, :].unsqueeze(1).broadcast_to([P, NT, E]), ALU.add))
                    after()
                    dve.sem_inc(past_dve, 1)
                    for i in range(NT):
                        link(dve.max(m8[:, i, :], mk[:, i, 0:E]))
                    after()
                    dve.sem_inc(past_dve, 1)
                    for i in range(NT):
                        link(dve.max_index(ix[:, i, :], m8[:, i, :], mk[:, i, 0:E]))
                    after()
                    link(dve.tensor_copy(ixf[:, :, :], ix[:, :, 0:TOP0]))
                    after()
                    io = iota0[:, :].unsqueeze(1).broadcast_to([P, NT, E])
                    link(dve.tensor_tensor(ex[:, :, 0:E], io, ixf[:, :, 0:1].broadcast_to([P, NT, E]), ALU.is_equal))
                    link(dve.tensor_tensor(mk[:, :, 0:E], io, ixf[:, :, 1:2].broadcast_to([P, NT, E]), ALU.is_equal))
                    after()
                    link(dve.tensor_tensor(ex[:, :, 0:E], ex[:, :, 0:E], mk[:, :, 0:E], ALU.add))
                    after()
                    link(dve.tensor_tensor(ex[:, :, 0:E], ex[:, :, 0:E], lg[:, :, 0:E], ALU.mult))
                    after()
                else:
                    E = E1
                    link(dve.tensor_copy(lg[:, :, :], ps[:, 2 + c, 0:NT * R1].rearrange("p (i e) -> p i e", i=NT)))
                    after()
                    dve.sem_inc(past_dve, 1)
                    for i in range(NT):
                        link(dve.max(m8[:, i, :], lg[:, i, 0:E]))
                    after()
                    dve.sem_inc(past_dve, 1)
                    for i in range(NT):
                        link(dve.match_replace(mk[:, i, 0:E], m8[:, i, :], lg[:, i, 0:E], TAKEN))
                    after()
                    link(dve.tensor_tensor(mk[:, :, 0:E], mk[:, :, 0:E], lg[:, :, 0:E], ALU.not_equal))
                    link(dve.tensor_tensor(ex[:, :, 0:E], lg[:, :, 0:E], m8[:, :, 0:1].broadcast_to([P, NT, E]), ALU.subtract))
                    after()
                    dve.wait_ge(route_exp, ROUTED_EXP(layer, chunk) + 1)
                    link(dve.tensor_tensor(ex[:, :, 0:E], ex[:, :, 0:E], mk[:, :, 0:E], ALU.mult))
                    link(dve.tensor_scalar(ex[:, :, E:R1], ex[:, :, E:R1], 1.0, None, ALU.add))
                    after()
                link(dve.tensor_reduce(rsum[:, :], ex[:, :, 0:E], AX.X, ALU.add))
                after()
                link(dve.reciprocal(rsum[:, :], rsum[:, :]))
                after()
                dve.wait_ge(route_turned, routed + 1)
                if layer in (F0A, F0B):
                    dve.memset(wr[:, :, E:E + 1], 1.0)
                else:
                    dve.reciprocal(wr[:, :, E:E + 1], ex[:, :, E:R1])
                dve.tensor_tensor(wr[:, :, 0:E], ex[:, :, 0:E], rsum[:, :].unsqueeze(2).broadcast_to([P, NT, E]),
                                  ALU.mult).then_inc(route_ready, 1)
                assert done[0] == (D0 if layer in (F0A, F0B) else D1), done

            def multiply(q, c):
                dve.wait_ge(up_ready, q + 1)
                dve.wait_ge(silu_done, q + 1 + RING)
                dve.wait_ge(weighted, q + 1)
                dve.tensor_tensor(prod[:, c, :], gact[:, c, :], ps[:, 6 + c, :], ALU.mult).then_inc(prod_done, 1)

            def hidden_lo(q, c):
                dve.wait_ge(hid_hi, q + 1)
                dve.wait_ge(down_done, q + 1)
                dve.tensor_tensor(iwl[:, c, :], iw[:, c, :], iwh[:, c, :], ALU.subtract).then_inc(hid_lo, 1)

            def ffn(layer):
                n = TILES[layer]
                centre(layer, 0, (0, 1))
                for pr in range(PAIRS_OF):
                    base = tiles_before(layer, pr)
                    scale(layer, 2 * pr, (0, 1))
                    for c in range(2):
                        dve.wait_ge(xn_hi, ROUTED[layer] * NBATCH + 2 * pr + c + 1)
                        dve.tensor_tensor(xnl[:, c, :, :], xn[:, c, :, :], xnh[:, c, :, :], ALU.subtract).then_inc(xn_lo, 1)
                    for c in range(2):
                        route(layer, 2 * pr + c, c)
                    with dve.Fori(0, n) as t:
                        for c in range(2):
                            multiply(2 * (base + t) + c, c)
                            hidden_lo(2 * (base + t) + c, c)
                    if pr < PAIRS_OF - 1:
                        centre(layer, 2 * pr + 2, (0, 1))
                    dve.wait_ge(down_done, 2 * (base + n) + RING)
                    for c in range(2):
                        for k in range(KT):
                            x = xT[:, k, 2 * pr + c, :]
                            dve.scalar_tensor_tensor(x, ps[:, 2 * c + k, :], 0.5, x, ALU.mult, ALU.add).then_inc(x_updated, 1)

            def attention():
                normalise_all(ATT)
                with dve.Fori(0, NBATCH) as b:
                    dve.wait_ge(qkv_ready, 4 * b + 1)
                    for m in range(HPT):
                        dve.tensor_scalar(kpad[:, m, :], ps[:, 2, :], headmask[:, m:m + 1], None, ALU.mult).then_inc(k_kept, 1)
                    for u in range(NU + 2):
                        U, r = NU * b + u, u % RING
                        if u < NU:
                            dve.wait_ge(score_ready, U + 1)
                            S = ps[:, 4 + r, :]
                            if len(UNITS[u]) == 1:
                                last = dve.tensor_reduce(mx[:, r, 0:1], S, AX.X, ALU.max)
                                np_ = 1
                            elif UNITS[u][1][3] == 2:
                                last = dve.tensor_reduce(mx[:, r, :], S.rearrange("p (h k) -> p h k", h=2), AX.X, ALU.max)
                                np_ = 2
                            else:
                                dve.tensor_reduce(mx[:, r, 0:1], S[:, 0:3 * P], AX.X, ALU.max)
                                last = dve.tensor_reduce(mx[:, r, 1:2], S[:, 3 * P:SEQ], AX.X, ALU.max)
                                np_ = 2
                            last.then_inc(max_found, 1)
                            dve.wait_ge(max_found, U + 1)
                            dve.wait_ge(prob_ready, U + 1)
                            dve.tensor_scalar(nb[:, r, 0:np_], mx[:, r, 0:np_], -SCALE, None, ALU.mult).then_inc(negmax, 1)
                        if u >= 2:
                            v, rv = U - 2, u % RING
                            dve.wait_ge(prob_turned, v + 1 + RING)
                            dve.wait_ge(pv_done, v + 1)
                            dve.tensor_copy(probT[:, rv, :], ps[:, 6 + rv, :]).then_inc(probT_kept, 1)
                        if u < NU and u % PER_PAIR == 3:
                            i = u // PER_PAIR
                            dve.wait_ge(e_hi, EPB * b + i + 1)
                            dve.tensor_tensor(wslot[:, i % WSLOTS, 1, :], ps[:, 0:2, :].rearrange("p k s -> p (k s)")[:, 0:REC],
                                              wslot[:, i % WSLOTS, 0, :], ALU.subtract).then_inc(e_lo, 1)
                    dve.wait_ge(prob_ready, NU * (b + 1) + RING)
                    dve.reciprocal(pinv[:, :, :], psums[:, :, :]).then_inc(inv_ready, 1)
                    dve.wait_ge(pv_done, NU * (b + 1) + RING)
                    dve.wait_ge(inv_ready, b + 2)
                    for m in range(2):
                        dve.tensor_tensor(osb[:, 2 * m:2 * m + 2, :].rearrange("p i (h d) -> p (i h) d", d=HD),
                                          ps[:, 2 + m, :].rearrange("p (g d) -> p g d", d=HD),
                                          pinv[:, 2 * m:2 * m + 2, :].rearrange("p i h -> p (i h)").unsqueeze(2).broadcast_to([P, 2 * HEADS, HD]),
                                          ALU.mult).then_inc(o_normed, 1)
                    dve.wait_ge(attn_out, b + 1)
                    for k in range(KT):
                        x = xT[:, k, b, :]
                        dve.tensor_tensor(x, ps[:, 6 + k, :], x, ALU.add).then_inc(x_updated, 1)

            def ssm():
                dve.memset(xpad[:, :, 0:TAPS - 1], 0.0)
                dve.memset(xact[:, (JT - 1) % RING, :], 0.0)
                normalise_all(SSM)
                for b in range(NBATCH):
                    dve.wait_ge(b_hi, b + 1)
                    dve.tensor_tensor(bl_all[:, b, :], ps[:, (2 * b) % 4, :], bh_all[:, b, :], ALU.subtract).then_inc(b_lo, 1)

                dve.wait_ge(xn_ready, KT * NBATCH * (SSM + 1))
                for j in range(JT):
                    for k in range(TAPS):
                        dve.tensor_scalar(convd[:, TAPS * j + k, :], ident[:], conv_w[:, j, k:k + 1], None, ALU.mult).then_inc(diagonals, 1)

                def split_c(N, r):
                    dve.wait_ge(proj_taken, JOBS * N + 4 + RING)
                    dve.tensor_tensor(iwl[:, r, :], ps[:, 5, :], iwh[:, r, :], ALU.subtract).then_inc(c_lo, 1)

                def one_plus(N):
                    dve.wait_ge(dt_exp, N + 1)
                    dve.tensor_scalar(sp_1, sp_e, 1.0, None, ALU.add).then_inc(dt_one, 1)
                    dve.wait_ge(dt_one, N + 1)
                    dve.scalar_tensor_tensor(sp_e, sp_1, -1.0, sp_e, ALU.add, ALU.subtract).then_inc(dt_lost, 1)

                def softplus_sum(N, r):
                    dve.wait_ge(dt_log, N + 1)
                    dve.scalar_tensor_tensor(dt[:, r, :], dt[:, r, :], 0.0, sp_l, ALU.max, ALU.add).then_inc(dt_sum, 1)

                def softplus_done(N, r):
                    dve.wait_ge(dt_sum, N + 1)
                    dve.wait_ge(dt_lost, N + 1)
                    dve.tensor_tensor(dt[:, r, :], dt[:, r, :], sp_e, ALU.subtract).then_inc(dt_done, 1)

                def add_out(J, b):
                    for k in range(KT):
                        x = xT[:, k, b, :]
                        dve.wait_ge(y_out, KT * J + k + 1)
                        dve.wait_ge(x_updated, x_before(SSM) + KT * J + 1)
                        dve.tensor_tensor(x, ps[:, 6 + k, :], x, ALU.add).then_inc(x_updated, 1)

                split_c(0, 0)
                one_plus(0)
                softplus_sum(0, 0)
                softplus_done(0, 0)
                with dve.Fori(0, NBATCH) as b:
                    for j in range(JT):
                        J, r = JT * b + j, j % RING
                        N, rn, jn = J + 1, (j + 1) % RING, (j + 1) % JT

                        def read_out(n):
                            s = STEPS * b + NST * j + n
                            dve.wait_ge(scanned, s + 1 + DECAYS)
                            dve.wait_ge(c_spread, s + 1 + RING)
                            dve.wait_ge(y_added, s + 1)
                            dve.tensor_tensor(hc[:, n % RING, :], hst[:, n % RING, :], ps[:, 2 + n % RING, :], ALU.mult).then_inc(hc_done, 1)

                        dve.wait_ge(dtx_done, J + 1)
                        for n in range(NST):
                            s, q = STEPS * b + NST * j + n, n % RING
                            dve.wait_ge(b_spread, s + 1)
                            dve.wait_ge(scanned, s - 1 + DECAYS)
                            dve.tensor_tensor(bx[:, q, :], dtx[:, r, :], ps[:, q, :], ALU.mult).then_inc(bx_done, 1)
                            if n:
                                read_out(n - 1)
                            dve.wait_ge(bx_done, s + 1 + RING)
                            dve.wait_ge(decay_ready, s + 1)
                            dve.wait_ge(hc_done, s + 1)
                            dve.tensor_tensor_scan(hst[:, q, :], da[:, n % DECAYS, :], bx[:, q, :], 0.0, ALU.mult, ALU.add).then_inc(scanned, 1)
                            if n == DVE_AT["add"]:
                                add_out(J, b if j else (b + NBATCH - 1) % NBATCH)
                            if n == DVE_AT["C"]:
                                split_c(N, rn)
                            if n == DVE_AT["one"]:
                                one_plus(N)
                            if n == DVE_AT["sum"]:
                                softplus_sum(N, rn)
                            if n == DVE_AT["done"]:
                                softplus_done(N, rn)
                        read_out(NST - 1)
                add_out(NBATCH * JT, NBATCH - 1)

            ffn(F0A)
            attention()
            ffn(F0B)
            ffn(F1A)
            ssm()
            ffn(F1B)
            for g in range(8):
                dve.wait_ge(out_turned, g + 1)
                dve.tensor_copy(outbuf[:, 2 * g:2 * g + 2, :].rearrange("p t c -> p (t c)"), ps[:, g % RING, :]).then_inc(out_kept, 1)


def kernel(**inputs):
    import numpy as np
    import concourse.bacc as bacc
    from concourse.bass_utils import run_bass_kernel_spmd

    nc = bacc.Bacc("TRN2", target_bir_lowering=False, num_devices=1)
    arrays, aps = {}, {}
    for name, value in inputs.items():
        v = np.ascontiguousarray(value)
        arrays[f"in_{name}"] = v
        aps[name] = nc.dram_tensor(f"in_{name}", v.shape, mybir.dt.from_np(v.dtype), kind="ExternalInput").ap()
    out = nc.dram_tensor("out", inputs["L0_attn_x"].shape, F32, kind="ExternalOutput").ap()
    macaron_kernel(nc, aps, out)
    r = run_bass_kernel_spmd(nc, [arrays], core_ids=[0])
    return r.results[0]["out"]
```
